# Optimizing a Trainium2 kernel written in Bass

```python
import numpy as np
import jax
import jax.numpy as jnp

def _softmax(x, axis=-1):
    return jax.nn.softmax(x, axis=axis)

def _gelu(x):
    return jax.nn.gelu(x, approximate=True)

def _silu(x):
    return jax.nn.silu(x)

def _sigmoid(x):
    return jax.nn.sigmoid(x)

def _layernorm(x, axis=-1, eps=1e-05):
    m = jnp.mean(x, axis=axis, keepdims=True)
    v = jnp.var(x, axis=axis, keepdims=True)
    return (x - m) / jnp.sqrt(v + eps)

def _scatter_add(tgt, idx, src, axis=0):
    return tgt.at[idx].add(src)

def _segment_sum(src, seg, n):
    return jax.ops.segment_sum(src, seg, n)
kernel_name = 'mk_hybrid_d1_jaxref_r4_68a8c7'

def setup_inputs(seed: int=0):
    np.random.seed(seed)
    _w = jnp.asarray

    def _L0_attn_a_setup():
        import jax, jax.numpy as jnp
        import numpy as np
        THETA = 10000.0
        NUM_HEADS = 16

        def _rope_tables(seq_len, d_k, dtype):
            exponent = jnp.arange(d_k // 2, dtype=jnp.float32) * (2.0 / d_k)
            inv_freq = THETA ** (-exponent)
            pos = jnp.arange(seq_len, dtype=jnp.float32)
            angles = pos[:, None] * inv_freq[None, :]
            return (jnp.cos(angles).astype(dtype), jnp.sin(angles).astype(dtype))

        def _apply_rope(x, cos, sin):
            x1 = x[..., 0::2]
            x2 = x[..., 1::2]
            r1 = x1 * cos - x2 * sin
            r2 = x1 * sin + x2 * cos
            return jnp.stack([r1, r2], axis=-1).reshape(x.shape)
        key = jax.random.key(seed)
        ks = jax.random.split(key, 5)
        B, N, D = (2, 1024, 256)
        std = (2.0 / (D + D)) ** 0.5
        return {'x': jax.random.normal(ks[0], (B, N, D), dtype=jnp.float32), 'Wq': jax.random.normal(ks[1], (D, D), dtype=jnp.float32) * std, 'Wk': jax.random.normal(ks[2], (D, D), dtype=jnp.float32) * std, 'Wv': jax.random.normal(ks[3], (D, D), dtype=jnp.float32) * std, 'Wo': jax.random.normal(ks[4], (D, D), dtype=jnp.float32) * std}
    _L0_attn_a_in = _L0_attn_a_setup()

    def _L0_attn_b_setup():
        import jax, jax.numpy as jnp
        import numpy as np
        HEADS = 16
        DIM_HEAD = 64
        key = jax.random.key(seed)
        k1, k2, k3, k4 = jax.random.split(key, 4)
        B, T, D = (4, 256, 256)
        x = jax.random.normal(k1, (B, T, D), dtype=jnp.float32)
        w_qkv = jax.random.normal(k2, (3 * HEADS * DIM_HEAD, D), dtype=jnp.float32) * (1.0 / np.sqrt(D))
        w_out = jax.random.normal(k3, (D, HEADS * DIM_HEAD), dtype=jnp.float32) * (1.0 / np.sqrt(HEADS * DIM_HEAD))
        rel_bias = jax.random.normal(k4, (2 * 256 - 1, HEADS), dtype=jnp.float32) * 0.02
        return {'x': x, 'w_qkv': w_qkv, 'w_out': w_out, 'rel_bias': rel_bias}
    _L0_attn_b_in = _L0_attn_b_setup()

    def _L0_ffn_setup():
        import jax, jax.numpy as jnp
        import numpy as np
        CAPACITY_FACTOR = 0.5
        NUM_HEADS = 16
        key = jax.random.key(seed)
        ks = jax.random.split(key, 6)
        B, N, D = (4, 1024, 256)
        s = 1.0 / np.sqrt(D)
        return {'token_inputs': jax.random.normal(ks[0], (B, N, D), jnp.float32), 'Wg': jax.random.normal(ks[1], (D, 1), jnp.float32) * s, 'Wq': jax.random.normal(ks[2], (D, D), jnp.float32) * s, 'Wk': jax.random.normal(ks[3], (D, D), jnp.float32) * s, 'Wv': jax.random.normal(ks[4], (D, D), jnp.float32) * s, 'Wo': jax.random.normal(ks[5], (D, D), jnp.float32) * s}
    _L0_ffn_in = _L0_ffn_setup()
    _d = {'L0_attn_a_x': _L0_attn_a_in['x'], 'L0_attn_a_Wq': _L0_attn_a_in['Wq'], 'L0_attn_a_Wk': _L0_attn_a_in['Wk'], 'L0_attn_a_Wv': _L0_attn_a_in['Wv'], 'L0_attn_a_Wo': _L0_attn_a_in['Wo'], 'L0_attn_b_w_qkv': _L0_attn_b_in['w_qkv'], 'L0_attn_b_w_out': _L0_attn_b_in['w_out'], 'L0_attn_b_rel_bias': _L0_attn_b_in['rel_bias'], 'L0_ffn_Wg': _L0_ffn_in['Wg'], 'L0_ffn_Wq': _L0_ffn_in['Wq'], 'L0_ffn_Wk': _L0_ffn_in['Wk'], 'L0_ffn_Wv': _L0_ffn_in['Wv'], 'L0_ffn_Wo': _L0_ffn_in['Wo']}
    _x0 = _d['L0_attn_a_x']
    _d['L0_attn_a_x'] = jax.random.normal(jax.random.fold_in(jax.random.key(seed), 1), (8, 512, 256), dtype=_x0.dtype)
    del _x0
    return _d

def reference(L0_attn_a_x, L0_attn_a_Wq, L0_attn_a_Wk, L0_attn_a_Wv, L0_attn_a_Wo, L0_attn_b_w_qkv, L0_attn_b_w_out, L0_attn_b_rel_bias, L0_ffn_Wg, L0_ffn_Wq, L0_ffn_Wk, L0_ffn_Wv, L0_ffn_Wo):

    def _L0_attn_a_ref(x, Wq, Wk, Wv, Wo):
        import jax, jax.numpy as jnp
        import numpy as np
        THETA = 10000.0
        NUM_HEADS = 16

        def _rope_tables(seq_len, d_k, dtype):
            exponent = jnp.arange(d_k // 2, dtype=jnp.float32) * (2.0 / d_k)
            inv_freq = THETA ** (-exponent)
            pos = jnp.arange(seq_len, dtype=jnp.float32)
            angles = pos[:, None] * inv_freq[None, :]
            return (jnp.cos(angles).astype(dtype), jnp.sin(angles).astype(dtype))

        def _apply_rope(x, cos, sin):
            x1 = x[..., 0::2]
            x2 = x[..., 1::2]
            r1 = x1 * cos - x2 * sin
            r2 = x1 * sin + x2 * cos
            return jnp.stack([r1, r2], axis=-1).reshape(x.shape)
        B, N, D = x.shape
        H = NUM_HEADS
        d_k = D // H

        def proj(W):
            y = jnp.einsum('oi,bni->bno', W, x)
            return y.reshape(B, N, H, d_k).transpose(0, 2, 1, 3)
        Q, K, V = (proj(Wq), proj(Wk), proj(Wv))
        cos, sin = _rope_tables(N, d_k, x.dtype)
        Q = _apply_rope(Q, cos, sin)
        K = _apply_rope(K, cos, sin)
        scores = jnp.einsum('bhnd,bhmd->bhnm', Q, K) / jnp.sqrt(jnp.asarray(d_k, x.dtype))
        causal = jnp.tril(jnp.ones((N, N), dtype=bool))
        scores = jnp.where(causal, scores, -jnp.inf)
        attn = jax.nn.softmax(scores, axis=-1)
        out = jnp.einsum('bhnm,bhmd->bhnd', attn, V)
        out = out.transpose(0, 2, 1, 3).reshape(B, N, D)
        return jnp.einsum('oi,bni->bno', Wo, out)

    def _L0_attn_b_ref(x, w_qkv, w_out, rel_bias):
        import jax, jax.numpy as jnp
        import numpy as np
        HEADS = 16
        DIM_HEAD = 64
        b, t, _ = x.shape
        h, dh = (HEADS, DIM_HEAD)
        scale = dh ** (-0.5)
        qkv = x @ w_qkv.T
        qkv = qkv.reshape(b, t, dh, 3, h).transpose(3, 0, 4, 1, 2)
        q, k, v = (qkv[0], qkv[1], qkv[2])
        scores = jnp.einsum('bhid,bhjd->bhij', q, k) * scale
        rel = jnp.arange(t)[None, :] - jnp.arange(t)[:, None] + (t - 1)
        bias = rel_bias[rel]
        scores = scores + bias.transpose(2, 0, 1)[None]
        attn = jax.nn.softmax(scores, axis=-1)
        out = jnp.einsum('bhij,bhjd->bhid', attn, v)
        out = out.transpose(0, 2, 1, 3).reshape(b, t, h * dh)
        return out @ w_out.T

    def _L0_ffn_ref(token_inputs, Wg, Wq, Wk, Wv, Wo):
        import jax, jax.numpy as jnp
        import numpy as np
        CAPACITY_FACTOR = 0.5
        NUM_HEADS = 16
        B, N, D = token_inputs.shape
        C = int(N * CAPACITY_FACTOR)
        H = NUM_HEADS
        dh = D // H
        gate = jax.nn.sigmoid((token_inputs @ Wg)[..., 0])
        _, idx = jax.lax.top_k(gate, C)
        attn_in = jnp.take_along_axis(token_inputs, idx[..., None], axis=1)
        q = (attn_in @ Wq).reshape(B, C, H, dh)
        k = (attn_in @ Wk).reshape(B, C, H, dh)
        v = (attn_in @ Wv).reshape(B, C, H, dh)
        scores = jnp.einsum('bqhd,bkhd->bhqk', q, k) / jnp.sqrt(jnp.float32(dh))
        attn = jax.nn.softmax(scores, axis=-1)
        o = jnp.einsum('bhqk,bkhd->bqhd', attn, v).reshape(B, C, D) @ Wo
        gate_sel = jnp.take_along_axis(gate, idx, axis=1)
        out = jnp.zeros_like(token_inputs)
        out = out.at[jnp.arange(B)[:, None], idx].set(o * gate_sel[..., None])
        return out
    x = L0_attn_a_x
    x = x + _L0_attn_a_ref(_layernorm(x, axis=-1), L0_attn_a_Wq, L0_attn_a_Wk, L0_attn_a_Wv, L0_attn_a_Wo)
    x = x + _L0_ffn_ref(_layernorm(x, axis=-1), L0_ffn_Wg, L0_ffn_Wq, L0_ffn_Wk, L0_ffn_Wv, L0_ffn_Wo)
    x = x + _L0_attn_b_ref(_layernorm(x, axis=-1), L0_attn_b_w_qkv, L0_attn_b_w_out, L0_attn_b_rel_bias)
    x = x + _L0_ffn_ref(_layernorm(x, axis=-1), L0_ffn_Wg, L0_ffn_Wq, L0_ffn_Wk, L0_ffn_Wv, L0_ffn_Wo)
    return x

_drawn_inputs = setup_inputs


def setup_inputs(seed=0):
    import zlib

    import numpy as np

    out = dict(_drawn_inputs(seed))
    spreads = {}
    factors = {'L0_attn_b_rel_bias': 35.359}
    for name, (base, spread) in spreads.items():
        noise = np.random.default_rng([zlib.crc32(name.encode()), seed]).standard_normal(out[name].shape)
        drawn = base * np.exp(spread * noise) if base else spread * noise
        out[name] = jnp.asarray(drawn.astype(out[name].dtype))
    for name, factor in factors.items():
        out[name] = (out[name] * factor).astype(out[name].dtype)
    return out
```

```python
from contextlib import ExitStack

import concourse.bass as bass
from concourse import mybir

F32 = mybir.dt.float32
BF16 = mybir.dt.bfloat16
ALU = mybir.AluOpType
ACT = mybir.ActivationFunctionType

P = 128
B, T, D = 8, 512, 256
NT, NC = T // P, D // P
H = 16
DH = D // H
DB = 64
CAP = T // 2
NS = CAP // P
GAP = 32
NG = H // 4
REL = 2 * 256 - 1
BAND = T + (NT - 1) * P
EPS = 1e-5
FAR = 1e30
SB = 4

CAUSAL, BIASED, FFN = "causal", "biased", "ffn"
LAYERS = (CAUSAL, FFN, BIASED, FFN)


class Ring:

    def __init__(self):
        self.n = 0

    def take(self):
        self.n += 1
        return self.n - 1


HELD = {CAUSAL: 3, BIASED: 2, FFN: 8}
AHEAD = {CAUSAL: 2, BIASED: 2, FFN: 6}
MASK_AHEAD = {CAUSAL: 2, FFN: 3}
NORM_LAG = {CAUSAL: 1, BIASED: 1, FFN: 3}
PT_HELD = {CAUSAL: 5, BIASED: 3, FFN: 6}
Q_HELD = {CAUSAL: 4, BIASED: 4, FFN: 8}
GROUP = {CAUSAL: 4, BIASED: 2, FFN: 4}


def attention_steps(layer):
    out = []
    ahead, lag, group = AHEAD[layer], NORM_LAG[layer], GROUP[layer]
    for n in range(H + ahead + 1):
        if layer is BIASED:
            if n == 0:
                out.append(("pair", 0))
            if n + 1 < H and (n + 1) % 2 == 0:
                out.append(("pair", (n + 1) // 2))
        else:
            more = MASK_AHEAD[layer]
            for m in range(more + 1) if n == 0 else range(n + more, n + more + 1):
                if m < H:
                    out.append(("mask", m))
        if n < H:
            out.append(("scores", n))
        if 0 <= n - lag < H:
            out.append(("norm", n - lag))
        h = n - ahead
        if 0 <= h < H:
            out.append(("turn", h))
        if h >= 1 and h % group == 0:
            out.append(("values", h // group - 1))
    return out


def hybrid_kernel(nc, x_in, wqk_a, wv_a, wo_a, w_b, wo_b, band_in, wg_f, wq_f, wk_f, wv_f, wo_f,
                  cos_in, sin_in, head_mask_in, pair_mask_in, out):
    with ExitStack() as ctx:
        def sb(name, shape, dt=F32):
            return ctx.enter_context(nc.sbuf_tensor(name, shape, dt))

        def sem(name):
            return ctx.enter_context(nc.semaphore(name))

        wqk = sb("wqk", [P, NC, 2 * D])
        wva = sb("wva", [P, NC, D])
        woa = sb("woa", [P, NG, D])
        wb = sb("wb", [P, NC, 3, H * DB])
        wob = sb("wob", [P, H * DB // P, D])
        band = sb("band", [P, H, BAND])
        wg = sb("wg", [P, D])
        wqf = sb("wqf", [P, NC, D])
        wkf = sb("wkf", [P, NC, D])
        wvf = sb("wvf", [P, NC, D])
        wof = sb("wof", [P, NG, D])
        cos_t = sb("cos_t", [P, NT, 2, DH])
        sin_t = sb("sin_t", [P, NT, 2, DH])
        head_mask = sb("head_mask", [P, 8])
        pair_mask = sb("pair_mask", [P, 2])
        ident = sb("ident", [P, P])
        hide = sb("hide", [P, T])
        before = sb("before", [P, P], BF16)
        ones = sb("ones", [P, P], BF16)
        slot_row = sb("slot_row", [P, CAP])
        slot_col = sb("slot_col", [P, NS])
        pow_half = sb("pow_half", [P, NT])

        x = sb("x", [P, NT, D])
        xn = sb("xn", [P, NT, D])
        xnT = sb("xnT", [P, NC, T])
        stats = sb("stats", [P, NT, 6])
        mv = sb("mv", [P, NT, 2])
        veps = sb("veps", [P, NT])
        rstd = sb("rstd", [P, NT])
        work = sb("work", [P, 8 * T])
        QT = sb("QT", [P, 3 * T])
        Qm = sb("Qm", [P, 4, T])
        Vpad = sb("Vpad", [P, NT, H, GAP])
        probs = sb("probs", [P, 8 * T])
        PT = sb("PT", [P, 5 * 10 * P])
        peak = sb("peak", [P, 8, NT])
        total = sb("total", [P, 8, NT])
        rtotal = sb("rtotal", [P, 8, NT])
        z = sb("z", [P, NT])
        gate = sb("gate", [P, NT])
        gate_row = sb("gate_row", [P, T])
        rank = sb("rank", [P, NT])

        qkr = work[:, 0:4 * T].rearrange("p (t n) -> p t n", t=NT)
        rope_c = work[:, 4 * T:6 * T].rearrange("p (b n) -> p b n", b=2)
        rope_s = work[:, 6 * T:8 * T].rearrange("p (b n) -> p b n", b=2)
        OTa = work[:, 0:NG * T].rearrange("p (g n) -> p g n", g=NG)
        OTb = work[:, :].rearrange("p (m n) -> p m n", m=8)
        OTf = work[:, 0:NG * CAP].rearrange("p (g n) -> p g n", g=NG)
        spread = work[:, 2 * T:4 * T].rearrange("p (s n) -> p s n", s=NS)
        pick = work[:, 4 * T:6 * T].rearrange("p (t n) -> p t n", t=NT)
        above = work[:, 6 * T:8 * T].bitcast(BF16).rearrange("p (t n) -> p t n", t=NT)
        of = work[:, 6 * T:7 * T].rearrange("p (s n) -> p s n", s=NS)
        xgT = work[:, 7 * T:8 * T].rearrange("p (c n) -> p c n", c=NC)
        QTa = QT[:, 0:2 * T].rearrange("p (c n) -> p c n", c=2)
        QTf = QT[:, 0:T].rearrange("p (c n) -> p c n", c=2)
        Vb = QT[:, :].rearrange("p (r t n) -> p r t n", r=3, t=NT)
        KT = xn[:, :, :].rearrange("p (c t) d -> p c (t d)", c=2)
        Qmf = Qm[:, :, :].rearrange("p r (e n) -> p (r e) n", e=2)
        KTf = KT[:, 0, :].rearrange("p (c n) -> p c n", c=2)

        ps_s = ctx.enter_context(nc.psum_tensor("ps_s", [P, SB, T], F32))
        ps_t = ctx.enter_context(nc.psum_tensor("ps_t", [P, SB, T], F32))

        w_early = sem("w_early")
        w_late = sem("w_late")
        consts = sem("consts")
        const_step = sem("const_step")
        x_loaded = sem("x_loaded")
        x_stored = sem("x_stored")
        s_full = sem("s_full")
        s_used = sem("s_used")
        t_full = sem("t_full")
        t_used = sem("t_used")
        stats_done = sem("stats_done")
        mv_done = sem("mv_done")
        veps_done = sem("veps_done")
        rstd_done = sem("rstd_done")
        xn_done = sem("xn_done")
        x_done = sem("x_done")
        rope_done = sem("rope_done")
        mask_done = sem("mask_done")
        exp_done = sem("exp_done")
        rtotal_done = sem("rtotal_done")
        norm_done = sem("norm_done")
        logit_done = sem("logit_done")
        sig_exp_done = sem("sig_exp_done")
        sig_sum_done = sem("sig_sum_done")
        gate_done = sem("gate_done")
        row_done = sem("row_done")
        tie_done = sem("tie_done")
        above_done = sem("above_done")
        rank_done = sem("rank_done")
        pick_done = sem("pick_done")
        batch_sems = range(s_full.num, pick_done.num + 1)

        NL = len(LAYERS)
        NHEADS = NL * H
        heads_before = [l * H for l in range(NL)]
        W_EARLY, W_LATE, CONSTS = 12 * 16, 3 * 16, 11

        def turned_by_vector(layer, k):
            return layer is FFN or layer is CAUSAL and k < 2

        s_ring, t_ring = Ring(), Ring()
        slots = {}
        for l, layer in enumerate(LAYERS):
            if layer is not FFN:
                slots[l, "xT"] = [t_ring.take() for _ in range(NC)]
            if layer is CAUSAL:
                slots[l, "qk"] = [s_ring.take() for _ in range(NT)]
                slots[l, "v"] = [t_ring.take() for _ in range(NT // 2)]
                slots[l, "qkT"] = [t_ring.take() for _ in range(4)]
            if layer is FFN:
                slots[l, "row"] = s_ring.take()
                slots[l, "rank"] = [s_ring.take() for _ in range(2)]
                slots[l, "gather"] = t_ring.take()
                slots[l, "q"] = t_ring.take(), t_ring.take()
                slots[l, "k"] = t_ring.take()
                slots[l, "v"] = s_ring.take()
            for what, n in attention_steps(layer):
                if what == "pair":
                    slots[l, "pair", n] = s_ring.take(), t_ring.take(), t_ring.take()
                if what == "scores":
                    slots[l, "scores", n] = [s_ring.take() for _ in range(1 if layer is FFN else NT)]
                if what == "turn":
                    slots[l, "turn", n] = [("s", s_ring.take()) if turned_by_vector(layer, k) else ("t", t_ring.take())
                                           for k in range(1 if layer is FFN else NT)]
                if what == "values":
                    slots[l, "values", n] = s_ring.take()
            if layer is FFN:
                slots[l, "o"] = t_ring.take()
            slots[l, "y"] = [s_ring.take() for _ in range(NT // 2)]
        NSS, NTS = s_ring.n, t_ring.n
        assert NSS % SB == 0 and NTS % SB == 0, (NSS, NTS)

        def s_bank(n):
            return ps_s[:, n % SB, :]

        def t_bank(n):
            return ps_t[:, n % SB, :]

        def widths(layer):
            return {CAUSAL: [P * (q + 1) for q in range(NT)], BIASED: [T] * NT, FFN: [CAP] * NS}[layer]

        units_before = []
        n_units = 0
        for layer in LAYERS:
            units_before.append(n_units)
            n_units += H * len(widths(layer))

        def unit(l, h, q):
            w = widths(LAYERS[l])
            o = (h % HELD[LAYERS[l]]) * sum(w) + sum(w[:q])
            return probs[:, o:o + w[q]]

        def pt(l, h, k):
            layer = LAYERS[l]
            if layer is FFN:
                o = (h % PT_HELD[layer]) * NS * CAP + k * CAP
                return PT[:, o:o + CAP]
            if layer is BIASED:
                o = (h % PT_HELD[layer]) * NT * T + k * T
                return PT[:, o:o + T]
            starts = [0, 4 * P, 7 * P, 9 * P, 10 * P]
            o = (h % PT_HELD[layer]) * starts[-1] + starts[k]
            return PT[:, o:o + starts[k + 1] - starts[k]]

        mask_before = {l: sum(H for k in range(l) if LAYERS[k] is not BIASED) for l in range(NL)}
        NMASK = sum(H for k in LAYERS if k is not BIASED)
        ffn_no = {l: sum(1 for k in range(l) if LAYERS[k] is FFN) for l in range(NL)}
        NF = 2

        xv = x_in.rearrange("b (t p) d -> b p t d", p=P)
        ov = out.rearrange("b (t p) d -> b p t d", p=P)
        with nc.Block() as first:
            @first.sync
            def _(sp):
                sp.dma_start(x[:], xv[0]).then_inc(x_loaded, 16)
                for dst, src in ((wqk, wqk_a), (cos_t, cos_in), (sin_t, sin_in), (wva, wv_a), (head_mask, head_mask_in),
                                 (pair_mask, pair_mask_in), (woa, wo_a), (wg, wg_f), (wqf, wq_f), (wkf, wk_f),
                                 (wvf, wv_f), (wof, wo_f)):
                    sp.dma_start(dst[:], src).then_inc(w_early, 16)
                sp.dma_start(band[:], band_in).then_inc(w_late, 16)
                sp.dma_start(wb[:], w_b).then_inc(w_late, 16)
                sp.dma_start(wob[:], wo_b).then_inc(w_late, 16)
                sp.sem_inc(x_stored, 16)
                sp.wait_ge(w_early, W_EARLY)

            @first.gpsimd
            def _(pool):
                g = nc.gpsimd
                steps = [0]

                def then(ins):
                    steps[0] += 1
                    ins.then_inc(const_step, 1)
                    pool.wait_ge(const_step, steps[0])

                then(g.memset(ident[:], 0.0))
                g.affine_select(out=ident[:], in_=ident[:], compare_op=ALU.not_equal, fill=1.0, base=0,
                                pattern=[[-1, P]], channel_multiplier=1).then_inc(consts, 1)
                then(g.memset(hide[:], 0.0))
                g.affine_select(out=hide[:, T - P:T], in_=hide[:, T - P:T], compare_op=ALU.is_ge, fill=FAR, base=0,
                                pattern=[[-1, P]], channel_multiplier=1).then_inc(consts, 1)
                then(g.memset(before[:], 1.0))
                g.affine_select(out=before[:], in_=before[:], compare_op=ALU.is_gt, fill=0.0, base=0,
                                pattern=[[1, P]], channel_multiplier=-1).then_inc(consts, 1)
                g.memset(ones[:], 1.0).then_inc(consts, 1)
                g.memset(pow_half[:], -0.5).then_inc(consts, 1)
                g.memset(Vpad[:], 0.0).then_inc(consts, 1)
                g.iota(slot_row[:], pattern=[[1, CAP]], base=0, channel_multiplier=0,
                       allow_small_or_imprecise_dtypes=True).then_inc(consts, 1)
                for s in range(NS):
                    g.iota(slot_col[:, s:s + 1], pattern=[[1, 1]], base=P * s, channel_multiplier=1,
                           allow_small_or_imprecise_dtypes=True).then_inc(consts, 1)
                pool.wait_ge(w_late, W_LATE)
                for h in range(H):
                    last = g.tensor_scalar(band[:, h, :], band[:, h, :], -1.0, 1.0, ALU.mult, ALU.mult)
                last.then_inc(consts, 2)
                pool.wait_ge(consts, CONSTS)

        with nc.Fori(0, B) as it:
            with nc.Block(no_gpsimd_drain=True) as block:
                @block.sync
                def _(sp):
                    sp.wait_ge(x_done, NL)
                    sp.dma_start(ov[it], xn[:]).then_inc(x_stored, 16)
                    sp.dma_start(x[:], xv[(it + 1) % B]).then_inc(x_loaded, 16)

                @block.gpsimd
                def _(pool):
                    g = nc.gpsimd
                    for l, layer in enumerate(LAYERS):
                        pool.wait_ge(mv_done, l + 1)
                        g.tensor_scalar(veps[:], mv[:, :, 1], 1.0, EPS, ALU.mult, ALU.add).then_inc(veps_done, 1)
                        pool.wait_ge(veps_done, l + 1)
                        g.tensor_tensor(rstd[:], veps[:], pow_half[:], ALU.pow).then_inc(rstd_done, 1)
                        if layer is CAUSAL:
                            for t in range(NT):
                                pool.wait_ge(s_used, slots[l, "qk"][t] + 1)
                                g.tensor_tensor(qkr[:, t, :], rope_c[:, t % 2, :], rope_s[:, t % 2, :],
                                                ALU.add).then_inc(rope_done, 1)
                        for what, n in attention_steps(layer):
                            if what == "mask":
                                if n == 0:
                                    last_q = slots[l, "qkT"][1] if layer is CAUSAL else slots[l, "q"][1]
                                    pool.wait_ge(t_used, last_q + 1)
                                if n >= Q_HELD[layer]:
                                    pool.wait_ge(s_full, slots[l, "scores", n - Q_HELD[layer]][-1] + 1)
                                src = QTa[:, n // 8, :] if layer is CAUSAL else QTf[:, n // 8, :]
                                dst = Qm[:, n % 4, :] if layer is CAUSAL else Qmf[:, n % 8, :]
                                g.tensor_scalar(dst, src, head_mask[:, n % 8:n % 8 + 1], 1.0, ALU.mult,
                                                ALU.mult).then_inc(mask_done, 1)
                            if what == "norm":
                                h = n
                                pool.wait_ge(rtotal_done, heads_before[l] + h + 1)
                                for q in range(len(widths(layer))):
                                    last = g.tensor_scalar(unit(l, h, q), unit(l, h, q), rtotal[:, h % 8, q:q + 1], 1.0,
                                                           ALU.mult, ALU.mult)
                                last.then_inc(norm_done, 1)

                @block.scalar
                def _(act):
                    a = nc.scalar

                    def full(n):
                        act.wait_ge(t_full, n + 1)

                    def exps(l, h):
                        layer = LAYERS[l]
                        for q in range(len(widths(layer))):
                            slot = slots[l, "scores", h][0 if layer is FFN else q]
                            if layer is not FFN or q == 0:
                                act.wait_ge(s_used, slot + 1)
                            a.activation(unit(l, h, q), unit(l, h, q), ACT.Exp, bias=peak[:, h % 8, q:q + 1], scale=-1.0,
                                         accum_out=total[:, h % 8, q:q + 1]).then_inc(exp_done, 1)

                    for l, layer in enumerate(LAYERS):
                        if layer is not FFN:
                            for c in range(NC):
                                full(slots[l, "xT"][c])
                                a.activation(xnT[:, c, :], t_bank(slots[l, "xT"][c]), ACT.Copy).then_inc(t_used, 1)
                        if layer is CAUSAL:
                            for i in range(NT // 2):
                                n = slots[l, "v"][i]
                                full(n)
                                a.activation(Vpad[:, 2 * i:2 * i + 2, :, 0:DH],
                                             t_bank(n).rearrange("p (t h d) -> p t h d", t=2, h=H),
                                             ACT.Copy).then_inc(t_used, 1)
                            for c in range(4):
                                n = slots[l, "qkT"][c]
                                full(n)
                                a.activation(QTa[:, c, :] if c < 2 else KT[:, c - 2, :], t_bank(n),
                                             ACT.Copy).then_inc(t_used, 1)
                        if layer is FFN:
                            act.wait_ge(logit_done, ffn_no[l] + 1)
                            a.activation(gate[:], z[:], ACT.Exp, scale=-1.0).then_inc(sig_exp_done, 1)
                            n = slots[l, "gather"]
                            full(n)
                            a.activation(xgT, t_bank(n).rearrange("p (c n) -> p c n", c=NC), ACT.Copy).then_inc(t_used, 1)
                            for m in range(2):
                                n = slots[l, "q"][m]
                                full(n)
                                a.activation(QTf[:, m, :], t_bank(n)[:, 0:CAP], ACT.Copy,
                                             scale=-float(DH) ** -0.5).then_inc(t_used, 1)
                            n = slots[l, "k"]
                            full(n)
                            a.activation(KTf, t_bank(n).rearrange("p (c n) -> p c n", c=2), ACT.Copy).then_inc(t_used, 1)
                        for what, n in attention_steps(layer):
                            if what == "pair":
                                _, ks, vs = slots[l, "pair", n]
                                full(ks)
                                a.activation(KT[:, n % 2, :], t_bank(ks), ACT.Copy).then_inc(t_used, 1)
                                full(vs)
                                if n >= 3:
                                    act.wait_ge(s_full, slots[l, "values", n - 3] + 1)
                                a.activation(Vb[:, n % 3], t_bank(vs).rearrange("p (t n) -> p t n", t=NT),
                                             ACT.Copy).then_inc(t_used, 1)
                            if what == "scores":
                                exps(l, n)
                            if what == "turn" and any(ring == "t" for ring, _ in slots[l, "turn", n]):
                                old = n - PT_HELD[layer]
                                if old >= 0:
                                    act.wait_ge(s_full, slots[l, "values", old // GROUP[layer]] + 1)
                                for k, (ring, m) in enumerate(slots[l, "turn", n]):
                                    if ring == "t":
                                        full(m)
                                        lo = k * P if layer is CAUSAL else 0
                                        a.activation(pt(l, n, k), t_bank(m)[:, lo:T], ACT.Copy).then_inc(t_used, 1)
                        if layer is FFN:
                            n = slots[l, "o"]
                            full(n)
                            a.activation(of, t_bank(n).rearrange("p (s n) -> p s n", s=NS), ACT.Copy).then_inc(t_used, 1)

                @block.vector
                def _(dve):
                    v = nc.vector

                    def full(n):
                        dve.wait_ge(s_full, n + 1)

                    for l, layer in enumerate(LAYERS):
                        if l == 0:
                            dve.wait_ge(x_loaded, it * 16 + 16)
                        else:
                            dve.wait_ge(x_done, l)
                        for t in range(NT):
                            last = v.bn_stats(stats[:, t, :], x[:, t, :])
                        last.then_inc(stats_done, 1)
                        dve.wait_ge(stats_done, l + 1)
                        for t in range(NT):
                            last = v.bn_aggr(mv[:, t, :], stats[:, t, :])
                        last.then_inc(mv_done, 1)
                        dve.wait_ge(mv_done, l + 1)
                        dve.wait_ge(rstd_done, l + 1)
                        if l == 0:
                            dve.wait_ge(x_stored, it * 16 + 16)
                        for t in range(NT):
                            last = v.tensor_scalar(xn[:, t, :], x[:, t, :], mv[:, t, 0:1], rstd[:, t:t + 1],
                                                   ALU.subtract, ALU.mult)
                        last.then_inc(xn_done, 1)

                        if layer is CAUSAL:
                            for t in range(NT):
                                n = slots[l, "qk"][t]
                                full(n)
                                if t >= 2:
                                    dve.wait_ge(rope_done, t - 1)
                                src = s_bank(n).rearrange("p (a h d) -> p a h d", a=2, h=H)
                                rc = rope_c[:, t % 2, :].rearrange("p (a h d) -> p a h d", a=2, h=H)
                                rs = rope_s[:, t % 2, :].rearrange("p (a h e two) -> p a h e two", a=2, h=H, two=2)
                                sw = s_bank(n).rearrange("p (a h e two) -> p a h e two", a=2, h=H, two=2)
                                st = sin_t[:, t].rearrange("p a (e two) -> p a e two", two=2)
                                for a in range(2):
                                    v.tensor_tensor(rc[:, a], src[:, a],
                                                    cos_t[:, t, a:a + 1, :].to_broadcast([P, H, DH]), ALU.mult)
                                    for odd in range(2):
                                        last = v.tensor_tensor(rs[:, a, :, :, odd], sw[:, a, :, :, 1 - odd],
                                                               st[:, a:a + 1, :, odd].to_broadcast([P, H, DH // 2]),
                                                               ALU.mult)
                                last.then_inc(s_used, 1)

                        if layer is FFN:
                            f = ffn_no[l]
                            dve.wait_ge(xn_done, l + 1)
                            for t in range(NT):
                                last = v.tensor_tensor_reduce(out=pick[:, t, :], in0=xn[:, t, :], in1=wg[:], scale=1.0,
                                                              scalar=0.0, op0=ALU.mult, op1=ALU.add,
                                                              accum_out=z[:, t:t + 1])
                            last.then_inc(logit_done, 1)
                            dve.wait_ge(sig_exp_done, f + 1)
                            v.tensor_scalar_add(z[:], gate[:], 1.0).then_inc(sig_sum_done, 1)
                            dve.wait_ge(sig_sum_done, f + 1)
                            v.reciprocal(gate[:], z[:]).then_inc(gate_done, 1)
                            n = slots[l, "row"]
                            full(n)
                            v.tensor_copy(gate_row[:], s_bank(n)).then_inc(s_used, 1)
                            dve.wait_ge(s_used, n + 1)
                            for t in range(NT):
                                own = slice(t * P, (t + 1) * P)
                                last = v.scalar_tensor_tensor(out=above[:, t, own], in0=gate_row[:, own],
                                                              scalar=gate[:, t:t + 1], in1=before[:],
                                                              op0=ALU.is_equal, op1=ALU.mult)
                            last.then_inc(tie_done, 1)
                            for t in range(NT):
                                if t > 0:
                                    v.tensor_scalar(above[:, t, 0:t * P], gate_row[:, 0:t * P], gate[:, t:t + 1], None,
                                                    ALU.is_lt)
                                if t < NT - 1:
                                    v.tensor_scalar(above[:, t, (t + 1) * P:T], gate_row[:, (t + 1) * P:T],
                                                    gate[:, t:t + 1], None, ALU.is_le)
                            dve.wait_ge(tie_done, f + 1)
                            for t in range(NT):
                                own = slice(t * P, (t + 1) * P)
                                last = v.scalar_tensor_tensor(out=above[:, t, own], in0=gate_row[:, own],
                                                              scalar=gate[:, t:t + 1], in1=above[:, t, own],
                                                              op0=ALU.is_lt, op1=ALU.add)
                            last.then_inc(above_done, 1)
                            rn, cn = slots[l, "rank"]
                            full(rn)
                            for s in range(NS):
                                last = v.scalar_tensor_tensor(out=spread[:, s, :], in0=s_bank(rn),
                                                              scalar=slot_col[:, s:s + 1], in1=gate_row[:],
                                                              op0=ALU.is_equal, op1=ALU.mult)
                            last.then_inc(s_used, 1)
                            full(cn)
                            v.tensor_copy(rank[:], s_bank(cn)[:, 0:NT]).then_inc(s_used, 1)
                            dve.wait_ge(s_used, cn + 1)
                            for t in range(NT):
                                last = v.tensor_scalar(pick[:, t, :], slot_row[:], rank[:, t:t + 1], None, ALU.is_equal)
                            last.then_inc(pick_done, 1)
                            n = slots[l, "v"]
                            full(n)
                            v.tensor_copy(Vpad[:, 0:NS, :, 0:DH],
                                          s_bank(n).rearrange("p (t h d) -> p t h d", t=NS, h=H)).then_inc(s_used, 1)

                        def inverse(h):
                            dve.wait_ge(exp_done, units_before[l] + (h + 1) * len(widths(layer)))
                            w = len(widths(layer))
                            v.reciprocal(rtotal[:, h % 8, 0:w], total[:, h % 8, 0:w]).then_inc(rtotal_done, 1)

                        for what, n in attention_steps(layer):
                            if what == "pair":
                                m = slots[l, "pair", n][0]
                                full(m)
                                for e in range(2):
                                    last = v.tensor_scalar(Qm[:, (2 * n + e) % 4, :], s_bank(m), pair_mask[:, e:e + 1],
                                                           None, ALU.mult)
                                last.then_inc(s_used, 1)
                            if what == "scores":
                                if n >= HELD[layer]:
                                    ring, m = slots[l, "turn", n - HELD[layer]][-1]
                                    dve.wait_ge(s_full if ring == "s" else t_full, m + 1)
                                for q, w in enumerate(widths(layer)):
                                    m = slots[l, "scores", n][0 if layer is FFN else q]
                                    if layer is not FFN or q == 0:
                                        dve.wait_ge(s_full, m + 1)
                                    if layer is FFN:
                                        src, add = s_bank(m)[:, q * CAP:(q + 1) * CAP], hide[:, 0:CAP]
                                    elif layer is CAUSAL:
                                        src, add = s_bank(m)[:, 0:w], hide[:, T - w:T]
                                    else:
                                        lo = (NT - 1 - q) * P
                                        src, add = s_bank(m), band[:, n, lo:lo + T]
                                    last = v.tensor_tensor_reduce(out=unit(l, n, q), in0=src, in1=add, scale=1.0,
                                                                  scalar=3e38, op0=ALU.add, op1=ALU.min,
                                                                  accum_out=peak[:, n % 8, q:q + 1])
                                    if layer is not FFN or q == NS - 1:
                                        last.then_inc(s_used, 1)
                            if what == "norm":
                                inverse(n)
                            if what == "turn" and any(ring == "s" for ring, _ in slots[l, "turn", n]):
                                old = n - PT_HELD[layer]
                                if old >= 0:
                                    dve.wait_ge(s_full, slots[l, "values", old // GROUP[layer]] + 1)
                                for k, (ring, m) in enumerate(slots[l, "turn", n]):
                                    if ring == "s":
                                        full(m)
                                        if layer is FFN:
                                            o = (n % PT_HELD[layer]) * NS * CAP
                                            dst = PT[:, o:o + NS * CAP]
                                        else:
                                            dst = pt(l, n, k)
                                        lo = k * P if layer is CAUSAL else 0
                                        v.tensor_copy(dst, s_bank(m)[:, lo:T]).then_inc(s_used, 1)
                            if what == "values":
                                m = slots[l, "values", n]
                                full(m)
                                dst = {CAUSAL: OTa, BIASED: OTb, FFN: OTf}[layer][:, n, :]
                                v.tensor_copy(dst, s_bank(m)[:, 0:CAP if layer is FFN else T]).then_inc(s_used, 1)

                        for i in range(NT // 2):
                            n = slots[l, "y"][i]
                            full(n)
                            dst = xn if l == NL - 1 else x
                            last = v.tensor_tensor(dst[:, 2 * i:2 * i + 2, :], x[:, 2 * i:2 * i + 2, :],
                                                   s_bank(n).rearrange("p (t d) -> p t d", t=2), ALU.add)
                            last.then_inc(s_used, 1)
                        dve.wait_ge(s_used, slots[l, "y"][-1] + 1)
                        dve.sem_inc(x_done, 1)

                @block.tensor
                def _(pe):
                    te = nc.tensor

                    def s_slot(n):
                        if n >= SB:
                            pe.wait_ge(s_used, n - SB + 1)
                        return s_bank(n)

                    def t_slot(n):
                        if n >= SB:
                            pe.wait_ge(t_used, n - SB + 1)
                        return t_bank(n)

                    def s_ready(n):
                        pe.wait_ge(s_used, n + 1)

                    def t_ready(n):
                        pe.wait_ge(t_used, n + 1)

                    def product(o, pairs):
                        for i, (w, r) in enumerate(pairs):
                            last = te.matmul(o, w, r, start=(i == 0), stop=(i == len(pairs) - 1))
                        return last

                    for l, layer in enumerate(LAYERS):
                        pe.wait_ge(xn_done, l + 1)
                        if layer is not FFN:
                            for c in range(NC):
                                o = t_slot(slots[l, "xT"][c])
                                for t in range(NT):
                                    last = te.transpose(o[:, t * P:(t + 1) * P], xn[:, t, c * P:(c + 1) * P], ident[:])
                                last.then_inc(t_full, 1)
                            t_ready(slots[l, "xT"][-1])
                        if layer is CAUSAL:
                            for t in range(NT):
                                o = s_slot(slots[l, "qk"][t])
                                product(o, [(xnT[:, c, t * P:(t + 1) * P], wqk[:, c, :])
                                            for c in range(NC)]).then_inc(s_full, 1)
                            for i in range(NT // 2):
                                o = t_slot(slots[l, "v"][i])
                                for j in range(2):
                                    t = 2 * i + j
                                    last = product(o[:, j * D:(j + 1) * D],
                                                   [(xnT[:, c, t * P:(t + 1) * P], wva[:, c, :]) for c in range(NC)])
                                last.then_inc(t_full, 1)
                            for c in range(4):
                                o = t_slot(slots[l, "qkT"][c])
                                for t in range(NT):
                                    if c == 0:
                                        pe.wait_ge(rope_done, t + 1)
                                    last = te.transpose(o[:, t * P:(t + 1) * P], qkr[:, t, c * P:(c + 1) * P], ident[:])
                                last.then_inc(t_full, 1)
                            t_ready(slots[l, "qkT"][-1])
                        if layer is FFN:
                            f = ffn_no[l]
                            pe.wait_ge(gate_done, f + 1)
                            o = s_slot(slots[l, "row"])
                            for t in range(NT):
                                last = te.transpose(o[:, t * P:(t + 1) * P], gate[:, t:t + 1].to_broadcast([P, P]), ident[:])
                            last.then_inc(s_full, 1)
                            pe.wait_ge(above_done, f + 1)
                            rn, cn = slots[l, "rank"]
                            product(s_slot(rn), [(ones[:], above[:, t, :]) for t in range(NT)]).then_inc(s_full, 1)
                            o = s_slot(cn)
                            for i in range(NT):
                                last = product(o[:, i:i + 1], [(above[:, t, i * P:(i + 1) * P], ones[:, 0:1])
                                                               for t in range(NT)])
                            last.then_inc(s_full, 1)
                            pe.wait_ge(pick_done, f + 1)
                            o = t_slot(slots[l, "gather"])
                            for c in range(NC):
                                last = product(o[:, c * CAP:(c + 1) * CAP], [(xn[:, t, c * P:(c + 1) * P], pick[:, t, :])
                                                                             for t in range(NT)])
                            last.then_inc(t_full, 1)
                            t_ready(slots[l, "gather"])
                            for m in range(2):
                                product(t_slot(slots[l, "q"][m])[:, 0:CAP],
                                        [(wqf[:, c, m * P:(m + 1) * P], xgT[:, c, :]) for c in range(NC)]).then_inc(t_full, 1)
                            o = t_slot(slots[l, "k"])
                            for m in range(2):
                                last = product(o[:, m * CAP:(m + 1) * CAP],
                                               [(wkf[:, c, m * P:(m + 1) * P], xgT[:, c, :]) for c in range(NC)])
                            last.then_inc(t_full, 1)
                            o = s_slot(slots[l, "v"])
                            for s in range(NS):
                                last = product(o[:, s * D:(s + 1) * D],
                                               [(xgT[:, c, s * P:(s + 1) * P], wvf[:, c, :]) for c in range(NC)])
                            last.then_inc(s_full, 1)
                            t_ready(slots[l, "k"])
                            s_ready(slots[l, "v"])

                        for what, n in attention_steps(layer):
                            if what == "pair":
                                qs, ks, vs = slots[l, "pair", n]
                                product(s_slot(qs), [(wb[:, c, 0, n * P:(n + 1) * P], xnT[:, c, :])
                                                     for c in range(NC)]).then_inc(s_full, 1)
                                product(t_slot(ks), [(wb[:, c, 1, n * P:(n + 1) * P], xnT[:, c, :])
                                                     for c in range(NC)]).then_inc(t_full, 1)
                                o = t_slot(vs)
                                for t in range(NT):
                                    last = product(o[:, t * P:(t + 1) * P],
                                                   [(xnT[:, c, t * P:(t + 1) * P], wb[:, c, 2, n * P:(n + 1) * P])
                                                    for c in range(NC)])
                                last.then_inc(t_full, 1)
                            if what == "scores":
                                if layer is BIASED:
                                    s_ready(slots[l, "pair", n // 2][0])
                                    t_ready(slots[l, "pair", n // 2][1])
                                    keys = KT[:, (n // 2) % 2, :]
                                else:
                                    pe.wait_ge(mask_done, mask_before[l] + n + 1)
                                    keys = KT[:, n // 8, :] if layer is CAUSAL else KTf[:, n // 8, :]
                                for q, w in enumerate(widths(layer)):
                                    m = slots[l, "scores", n][0 if layer is FFN else q]
                                    if layer is FFN:
                                        o = (s_slot(m) if q == 0 else s_bank(m))[:, q * CAP:(q + 1) * CAP]
                                    else:
                                        o = s_slot(m)[:, 0:w]
                                    qs = Qmf[:, n % 8, :] if layer is FFN else Qm[:, n % 4, :]
                                    last = te.matmul(o, qs[:, q * P:(q + 1) * P], keys[:, 0:w], start=True, stop=True)
                                    if layer is not FFN or q == NS - 1:
                                        last.then_inc(s_full, 1)
                            if what == "turn":
                                pe.wait_ge(norm_done, heads_before[l] + n + 1)
                                for k, (ring, m) in enumerate(slots[l, "turn", n]):
                                    o = s_slot(m) if ring == "s" else t_slot(m)
                                    if layer is FFN:
                                        blocks = [(q, i) for i in range(NS) for q in range(NS)]
                                    else:
                                        blocks = [(q, k) for q in range(k if layer is CAUSAL else 0, NT)]
                                    for q, i in blocks:
                                        at = (i * CAP if layer is FFN else 0) + q * P
                                        last = te.transpose(o[:, at:at + P], unit(l, n, q)[:, i * P:(i + 1) * P],
                                                            ident[:])
                                    last.then_inc(s_full if ring == "s" else t_full, 1)
                            if what == "values":
                                size = GROUP[layer]
                                heads = range(size * n, size * n + size)
                                for ring in "st":
                                    m = [m for r, m in slots[l, "turn", heads[-1]] if r == ring]
                                    if m:
                                        (s_ready if ring == "s" else t_ready)(m[-1])
                                m = slots[l, "values", n]
                                o = s_slot(m)
                                if layer is BIASED:
                                    t_ready(slots[l, "pair", n][2])
                                rows = P // size
                                for k in range(NS if layer is FFN else NT):
                                    for e, h in enumerate(heads):
                                        lo = k * P if layer is CAUSAL else 0
                                        hi = CAP if layer is FFN else T
                                        w = Vb[:, n % 3, k, e * DB:(e + 1) * DB] if layer is BIASED else Vpad[:, k, h, :]
                                        last = te.matmul(o[e * rows:(e + 1) * rows, lo:hi], w, pt(l, h, k), start=(k == 0),
                                                         stop=(k == (NS if layer is FFN else NT) - 1))
                                last.then_inc(s_full, 1)

                        s_ready(slots[l, "values", H // GROUP[layer] - 1])
                        if layer is FFN:
                            o = t_slot(slots[l, "o"])
                            for s in range(NS):
                                last = product(o[:, s * D:(s + 1) * D],
                                               [(OTf[:, g, s * P:(s + 1) * P], wof[:, g, :]) for g in range(NG)])
                            last.then_inc(t_full, 1)
                            t_ready(slots[l, "o"])
                        for i in range(NT // 2):
                            o = s_slot(slots[l, "y"][i])
                            for j in range(2):
                                cols = slice((2 * i + j) * P, (2 * i + j + 1) * P)
                                if layer is FFN:
                                    pairs = [(spread[:, s, cols], of[:, s, :]) for s in range(NS)]
                                elif layer is CAUSAL:
                                    pairs = [(OTa[:, g, cols], woa[:, g, :]) for g in range(NG)]
                                else:
                                    pairs = [(OTb[:, m, cols], wob[:, m, :]) for m in range(H * DB // P)]
                                last = product(o[:, j * D:(j + 1) * D], pairs)
                            last.then_inc(s_full, 1)


            nc.all_engine_barrier(sems_to_clear=batch_sems)
        with nc.Block() as end:

            @end.sync
            def _(sp):
                sp.wait_ge(x_stored, 16 * (B + 1))
                sp.wait_ge(x_loaded, 16 * (B + 1))


def kernel(L0_attn_a_x, L0_attn_a_Wq, L0_attn_a_Wk, L0_attn_a_Wv, L0_attn_a_Wo, L0_attn_b_w_qkv, L0_attn_b_w_out,
           L0_attn_b_rel_bias, L0_ffn_Wg, L0_ffn_Wq, L0_ffn_Wk, L0_ffn_Wv, L0_ffn_Wo):
    import numpy as np
    import concourse.bacc as bacc
    from concourse.bass_utils import run_bass_kernel_spmd

    def chunks(w):
        w = np.asarray(w)
        return np.ascontiguousarray(w.reshape(-1, P, w.shape[-1]).transpose(1, 0, 2))

    def gapped(w):
        w = np.asarray(w)
        g = np.zeros((H, GAP, D), w.dtype)
        g[:, :DH] = w.reshape(H, DH, D)
        return chunks(g.reshape(H * GAP, D))

    inv = np.float32(10000.0) ** (-(np.arange(DH // 2, dtype=np.float32) * np.float32(2.0 / DH)))
    angle = np.arange(T, dtype=np.float32)[:, None] * inv[None, :].astype(np.float32)
    cos = np.repeat(np.cos(angle), 2, axis=1).astype(np.float32)
    sin = np.stack([-np.sin(angle), np.sin(angle)], axis=-1).reshape(T, DH).astype(np.float32)
    scale = np.array([-float(DH) ** -0.5, 1.0], np.float32)[None, :, None]
    cos2 = np.ascontiguousarray((cos[:, None, :] * scale).reshape(NT, P, 2, DH).transpose(1, 0, 2, 3))
    sin2 = np.ascontiguousarray((sin[:, None, :] * scale).reshape(NT, P, 2, DH).transpose(1, 0, 2, 3))
    head_mask = (np.arange(P)[:, None] // DH == np.arange(8)[None, :]).astype(np.float32)
    pair_mask = (np.arange(P)[:, None] // DB == np.arange(2)[None, :]).astype(np.float32) * np.float32(-float(DB) ** -0.5)

    at = np.minimum(np.arange(BAND)[None, :] - np.arange(P)[:, None] + P - 1, REL - 1)
    band = np.ascontiguousarray(np.asarray(L0_attn_b_rel_bias).T[:, at].transpose(1, 0, 2))

    w_b = np.asarray(L0_attn_b_w_qkv).reshape(DB, 3, H, D).transpose(3, 1, 2, 0).reshape(D, 3 * H * DB)
    w_b = chunks(w_b).reshape(P, NC, 3, H * DB)
    wqk_a = chunks(np.concatenate([np.asarray(L0_attn_a_Wq).T, np.asarray(L0_attn_a_Wk).T], axis=1))
    arrays = {
        "x": np.asarray(L0_attn_a_x),
        "wqk_a": wqk_a,
        "wv_a": chunks(np.asarray(L0_attn_a_Wv).T),
        "wo_a": gapped(np.asarray(L0_attn_a_Wo).T),
        "w_b": w_b,
        "wo_b": chunks(np.asarray(L0_attn_b_w_out).T),
        "band": band,
        "wg_f": np.ascontiguousarray(np.broadcast_to(np.asarray(L0_ffn_Wg).reshape(1, D), (P, D))),
        "wq_f": chunks(L0_ffn_Wq),
        "wk_f": chunks(L0_ffn_Wk),
        "wv_f": chunks(L0_ffn_Wv),
        "wo_f": gapped(L0_ffn_Wo),
        "cos": cos2,
        "sin": sin2,
        "head_mask": head_mask,
        "pair_mask": pair_mask,
    }
    nc = bacc.Bacc("TRN2", target_bir_lowering=False, num_devices=1)
    ins = {f"in_{k}": np.ascontiguousarray(a) for k, a in arrays.items()}
    aps = [nc.dram_tensor(k, a.shape, mybir.dt.from_np(a.dtype), kind="ExternalInput").ap() for k, a in ins.items()]
    out = nc.dram_tensor("out", (B, T, D), F32, kind="ExternalOutput").ap()
    hybrid_kernel(nc, *aps, out)
    r = run_bass_kernel_spmd(nc, [ins], core_ids=[0])
    return r.results[0]["out"]
```

```python
from contextlib import ExitStack

import concourse.bass as bass
from concourse import mybir

F32 = mybir.dt.float32
F32R = mybir.dt.float32r
BF16 = mybir.dt.bfloat16
ALU = mybir.AluOpType
ACT = mybir.ActivationFunctionType

P = 128
B, T, D = 8, 512, 256
NT, NC = T // P, D // P
H = 16
DH = D // H
DB = 64
CAP = T // 2
NS = CAP // P
GAP = 32
NG = H // 4
REL = 2 * 256 - 1
BAND = T + (NT - 1) * P
BANDS = 4
EPS = 1e-5
FAR = 1e30
SB = 4

CAUSAL, BIASED, FFN = "causal", "biased", "ffn"
LAYERS = (CAUSAL, FFN, BIASED, FFN)


class Ring:

    def __init__(self):
        self.n = 0

    def take(self):
        self.n += 1
        return self.n - 1


HELD = {CAUSAL: 3, BIASED: 3, FFN: 8}
AHEAD = {CAUSAL: 2, BIASED: 3, FFN: 6}
MASK_AHEAD = {CAUSAL: 2, FFN: 3}
NORM_LAG = {CAUSAL: 1, BIASED: 1, FFN: 3}
PT_HELD = {CAUSAL: 5, BIASED: 3, FFN: 6}
Q_HELD = {CAUSAL: 4, BIASED: 4, FFN: 8}
GROUP = {CAUSAL: 4, BIASED: 2, FFN: 4}


TURN_FIRST = (BIASED,)


def attention_steps(layer):
    out = []
    ahead, lag, group = AHEAD[layer], NORM_LAG[layer], GROUP[layer]
    for n in range(H + ahead + 1):
        if layer is BIASED:
            if n == 0:
                out.append(("pair", 0))
            if n % 2 == 0 and n + 2 < H:
                out.append(("pair", n // 2 + 1))
        else:
            more = MASK_AHEAD[layer]
            for m in range(more + 1) if n == 0 else range(n + more, n + more + 1):
                if m < H:
                    out.append(("mask", m))
        h = n - ahead
        if 0 <= h < H and layer in TURN_FIRST:
            out.append(("turn", h))
        if n < H:
            out.append(("scores", n))
        if 0 <= n - lag < H:
            out.append(("norm", n - lag))
        if 0 <= h < H and layer not in TURN_FIRST:
            out.append(("turn", h))
        if h >= 1 and h % group == 0:
            out.append(("values", h // group - 1))
    return out


def hybrid_kernel(nc, x_in, wqk_a, wv_a, wo_a, w_b, wo_b, band_in, wg_f, wq_f, wk_f, wv_f, wo_f,
                  cos_in, sin_in, head_mask_in, out):
    with ExitStack() as ctx:
        def sb(name, shape, dt=F32):
            return ctx.enter_context(nc.sbuf_tensor(name, shape, dt))

        def sem(name):
            return ctx.enter_context(nc.semaphore(name))

        wqk = sb("wqk", [P, NC, 2 * D])
        wva = sb("wva", [P, NC, D])
        woa = sb("woa", [P, NG, D])
        wb = sb("wb", [P, NC, 3, H * DB])
        wob = sb("wob", [P, H * DB // P, D])
        wg = sb("wg", [P, D])
        wqf = sb("wqf", [P, NC, D])
        wkf = sb("wkf", [P, NC, D])
        wvf = sb("wvf", [P, NC, D])
        wof = sb("wof", [P, NG, D])
        cos_t = sb("cos_t", [P, NT, 2, DH])
        sin_t = sb("sin_t", [P, NT, 2, DH])
        head_mask = sb("head_mask", [P, 8])
        ident = sb("ident", [P, P])
        hide = sb("hide", [P, T])
        before = sb("before", [P, P], BF16)
        ones = sb("ones", [P, P], BF16)
        slot_row = sb("slot_row", [P, CAP])
        slot_col = sb("slot_col", [P, NS])

        xin = sb("xin", [P, NT, D])
        x = sb("x", [P, NT, D])
        xn = sb("xn", [P, NT, D])
        xnT = sb("xnT", [P, NC, T])
        stats = sb("stats", [P, NT, 6])
        mv = sb("mv", [P, NT, 2])
        veps = sb("veps", [P, NT])
        rstd = sb("rstd", [P, NT])
        pow_half = sb("pow_half", [P, NT])
        work = sb("work", [P, 8 * T])
        QT = sb("QT", [P, 2 * T])
        Qparts = sb("Qparts", [P, 4, T], F32R)
        Kparts = sb("Kparts", [P, 2, 2, 2, T], F32R)
        Vb = sb("Vb", [P, 4, NT, P])
        band = sb("band", [P, BANDS, BAND])
        Vpad = sb("Vpad", [P, NT, H, GAP])
        probs = sb("probs", [P, 12 * T])
        PT = sb("PT", [P, 5 * 10 * P])
        peak = sb("peak", [P, 8, NT])
        total = sb("total", [P, 8, NT])
        rtotal = sb("rtotal", [P, 8, NT])
        z = sb("z", [P, NT])
        gate = sb("gate", [P, NT])
        gate_row = sb("gate_row", [P, T])
        rank = sb("rank", [P, NT])
        tie = sb("tie", [P, NT, P], BF16)
        logit_products = xnT[:, :, :].rearrange("p c (e d) -> p (c e) d", d=D)

        qkr = work[:, 0:4 * T].rearrange("p (t n) -> p t n", t=NT)
        rope_c = work[:, 4 * T:6 * T].rearrange("p (b n) -> p b n", b=2)
        rope_s = work[:, 6 * T:8 * T].rearrange("p (b n) -> p b n", b=2)
        OTa = work[:, 0:NG * T].rearrange("p (g n) -> p g n", g=NG)
        OTb = work[:, :].rearrange("p (m n) -> p m n", m=8)
        OTf = work[:, 0:NG * CAP].rearrange("p (g n) -> p g n", g=NG)
        spread = work[:, 2 * T:4 * T].rearrange("p (s n) -> p s n", s=NS)
        pick = work[:, 4 * T:6 * T].rearrange("p (t n) -> p t n", t=NT)
        above = work[:, 6 * T:8 * T].bitcast(BF16).rearrange("p (t n) -> p t n", t=NT)
        of = work[:, 6 * T:7 * T].rearrange("p (s n) -> p s n", s=NS)
        xgT = work[:, 7 * T:8 * T].rearrange("p (c n) -> p c n", c=NC)
        QTa = QT[:, :].rearrange("p (c n) -> p c n", c=2)
        QTf = QT[:, 0:T].rearrange("p (c n) -> p c n", c=2)
        Qm = Vb[:, :, :, :].rearrange("p r t n -> p r (t n)")
        KT = xn[:, :, :].rearrange("p (c t) d -> p c (t d)", c=2)
        Qmf = Vb[:, :, :, :].rearrange("p r (e u) n -> p (r e) (u n)", e=2)
        KTf = KT[:, 0, :].rearrange("p (c n) -> p c n", c=2)

        ps_s = ctx.enter_context(nc.psum_tensor("ps_s", [P, SB, T], F32))
        ps_t = ctx.enter_context(nc.psum_tensor("ps_t", [P, SB, T], F32))

        w_early = sem("w_early")
        w_late = sem("w_late")
        consts = sem("consts")
        const_step = sem("const_step")
        x_loaded = sem("x_loaded")
        x_stored = sem("x_stored")
        s_full = sem("s_full")
        s_used = sem("s_used")
        t_full = sem("t_full")
        t_used = sem("t_used")
        stats_done = sem("stats_done")
        mv_done = sem("mv_done")
        veps_done = sem("veps_done")
        rstd_done = sem("rstd_done")
        xn_done = sem("xn_done")
        x_done = sem("x_done")
        rope_done = sem("rope_done")
        mask_done = sem("mask_done")
        peak_done = sem("peak_done")
        exp_done = sem("exp_done")
        rtotal_done = sem("rtotal_done")
        norm_done = sem("norm_done")
        logit_done = sem("logit_done")
        sig_exp_done = sem("sig_exp_done")
        sig_sum_done = sem("sig_sum_done")
        gate_done = sem("gate_done")
        row_done = sem("row_done")
        above_done = sem("above_done")
        rank_done = sem("rank_done")
        pick_done = sem("pick_done")
        q_high_done = sem("q_high_done")
        k_high_done = sem("k_high_done")
        k_parts_done = sem("k_parts_done")
        band_loaded = [sem(f"band_loaded{i}") for i in range(BANDS)]
        batch_sems = range(s_full.num, band_loaded[-1].num + 1)

        NL = len(LAYERS)
        NHEADS = NL * H
        heads_before = [l * H for l in range(NL)]
        W_EARLY, W_LATE, CONSTS = 11 * 16, 2 * 16, 9

        def turned_by_vector(layer, k):
            return layer is FFN or layer is CAUSAL and k < 2

        s_ring, t_ring = Ring(), Ring()
        slots = {}
        for l, layer in enumerate(LAYERS):
            if layer is not FFN:
                slots[l, "xT"] = [t_ring.take() for _ in range(NC)]
            if layer is CAUSAL:
                slots[l, "qk"] = [s_ring.take() for _ in range(NT)]
                slots[l, "v"] = [t_ring.take() for _ in range(NT // 2)]
                slots[l, "qkT"] = [t_ring.take() for _ in range(4)]
            if layer is FFN:
                slots[l, "row"] = s_ring.take()
                slots[l, "rank"] = [s_ring.take() for _ in range(2)]
                slots[l, "gather"] = t_ring.take()
                slots[l, "q"] = t_ring.take(), t_ring.take()
                slots[l, "k"] = t_ring.take()
                slots[l, "v"] = s_ring.take()
            for what, n in attention_steps(layer):
                if what == "pair":
                    slots[l, "pair", n] = s_ring.take(), t_ring.take(), t_ring.take()
                if what == "scores":
                    slots[l, "scores", n] = [s_ring.take() for _ in range(1 if layer is FFN else NT)]
                if what == "turn":
                    slots[l, "turn", n] = [("s", s_ring.take()) if turned_by_vector(layer, k) else ("t", t_ring.take())
                                           for k in range(1 if layer is FFN else NT)]
                if what == "values":
                    slots[l, "values", n] = s_ring.take()
            if layer is FFN:
                slots[l, "o"] = t_ring.take()
            slots[l, "y"] = [s_ring.take() for _ in range(NT // 2)]
        NSS, NTS = s_ring.n, t_ring.n
        assert NSS % SB == 0 and NTS % SB == 0, (NSS, NTS)

        def s_bank(n):
            return ps_s[:, n % SB, :]

        def t_bank(n):
            return ps_t[:, n % SB, :]

        def widths(layer):
            return {CAUSAL: [P * (q + 1) for q in range(NT)], BIASED: [T] * NT, FFN: [CAP] * NS}[layer]

        units_before = []
        n_units = 0
        for layer in LAYERS:
            units_before.append(n_units)
            n_units += H * len(widths(layer))

        def unit(l, h, q):
            w = widths(LAYERS[l])
            o = (h % HELD[LAYERS[l]]) * sum(w) + sum(w[:q])
            return probs[:, o:o + w[q]]

        def pt(l, h, k):
            layer = LAYERS[l]
            if layer is FFN:
                o = (h % PT_HELD[layer]) * NS * CAP + k * CAP
                return PT[:, o:o + CAP]
            if layer is BIASED:
                o = (h % PT_HELD[layer]) * NT * T + k * T
                return PT[:, o:o + T]
            starts = [0, 4 * P, 7 * P, 9 * P, 10 * P]
            o = (h % PT_HELD[layer]) * starts[-1] + starts[k]
            return PT[:, o:o + starts[k + 1] - starts[k]]

        mask_before = {l: sum(H for k in range(l) if LAYERS[k] is not BIASED) for l in range(NL)}
        NMASK = sum(H for k in LAYERS if k is not BIASED)
        ffn_no = {l: sum(1 for k in range(l) if LAYERS[k] is FFN) for l in range(NL)}
        NF = 2

        xv = x_in.rearrange("b (t p) d -> b p t d", p=P)
        ov = out.rearrange("b (t p) d -> b p t d", p=P)
        with nc.Block() as first:
            @first.sync
            def _(sp):
                sp.dma_start(xin[:], xv[0]).then_inc(x_loaded, 16)
                for dst, src in ((wqk, wqk_a), (cos_t, cos_in), (sin_t, sin_in), (wva, wv_a), (head_mask, head_mask_in),
                                 (woa, wo_a), (wg, wg_f), (wqf, wq_f), (wkf, wk_f), (wvf, wv_f), (wof, wo_f)):
                    sp.dma_start(dst[:], src).then_inc(w_early, 16)
                sp.dma_start(wb[:], w_b).then_inc(w_late, 16)
                sp.dma_start(wob[:], wo_b).then_inc(w_late, 16)
                sp.sem_inc(x_stored, 16)
                sp.wait_ge(w_early, W_EARLY)

            @first.gpsimd
            def _(pool):
                g = nc.gpsimd
                steps = [0]

                def then(ins):
                    steps[0] += 1
                    ins.then_inc(const_step, 1)
                    pool.wait_ge(const_step, steps[0])

                then(g.memset(ident[:], 0.0))
                g.affine_select(out=ident[:], in_=ident[:], compare_op=ALU.not_equal, fill=1.0, base=0,
                                pattern=[[-1, P]], channel_multiplier=1).then_inc(consts, 1)
                then(g.memset(hide[:], 0.0))
                g.affine_select(out=hide[:, T - P:T], in_=hide[:, T - P:T], compare_op=ALU.is_ge, fill=FAR, base=0,
                                pattern=[[-1, P]], channel_multiplier=1).then_inc(consts, 1)
                then(g.memset(before[:], 1.0))
                g.affine_select(out=before[:], in_=before[:], compare_op=ALU.is_gt, fill=0.0, base=0,
                                pattern=[[1, P]], channel_multiplier=-1).then_inc(consts, 1)
                g.memset(ones[:], 1.0).then_inc(consts, 1)
                g.memset(pow_half[:], -0.5).then_inc(consts, 1)
                g.memset(Vpad[:], 0.0).then_inc(consts, 1)
                g.iota(slot_row[:], pattern=[[1, CAP]], base=0, channel_multiplier=0,
                       allow_small_or_imprecise_dtypes=True).then_inc(consts, 1)
                for s in range(NS):
                    g.iota(slot_col[:, s:s + 1], pattern=[[1, 1]], base=P * s, channel_multiplier=1,
                           allow_small_or_imprecise_dtypes=True).then_inc(consts, 1)
                pool.wait_ge(consts, CONSTS)

        with nc.Fori(0, B) as it:
            with nc.Block(no_gpsimd_drain=True) as block:
                @block.sync
                def _(sp):
                    def load_band(n):
                        sp.dma_start(band[:, n % BANDS, :], band_in[n]).then_inc(band_loaded[n % BANDS], 16)

                    for n in range(BANDS):
                        load_band(n)
                    sp.wait_ge(s_used, slots[0, "y"][-1] + 1)
                    sp.dma_start(xin[:], xv[(it + 1) % B]).then_inc(x_loaded, 16)
                    for n in range(BANDS, H):
                        sp.wait_ge(s_used, slots[LAYERS.index(BIASED), "scores", n - BANDS][-1] + 1)
                        load_band(n)
                    sp.wait_ge(x_done, 1)
                    sp.dma_start(ov[it], x[:]).then_inc(x_stored, 16)

                @block.gpsimd
                def _(pool):
                    g = nc.gpsimd

                    def inverse_deviations(l):
                        for i in range(2):
                            pool.wait_ge(veps_done, 2 * l + i + 1)
                            g.tensor_tensor(rstd[:, 2 * i:2 * i + 2], veps[:, 2 * i:2 * i + 2], pow_half[:, 0:2],
                                            ALU.pow).then_inc(rstd_done, 1)

                    for l, layer in enumerate(LAYERS):
                        inverse_deviations(l)
                        if layer is CAUSAL:
                            for t in range(NT):
                                pool.wait_ge(s_used, slots[l, "qk"][t] + 1)
                                g.tensor_tensor(qkr[:, t, :], rope_c[:, t % 2, :], rope_s[:, t % 2, :],
                                                ALU.add).then_inc(rope_done, 1)
                        for what, n in attention_steps(layer):
                            if what == "mask":
                                if n == 0:
                                    last_q = slots[l, "qkT"][1] if layer is CAUSAL else slots[l, "q"][1]
                                    pool.wait_ge(t_used, last_q + 1)
                                if n >= Q_HELD[layer]:
                                    pool.wait_ge(s_full, slots[l, "scores", n - Q_HELD[layer]][-1] + 1)
                                src = QTa[:, n // 8, :] if layer is CAUSAL else QTf[:, n // 8, :]
                                dst = Qm[:, n % 4, :] if layer is CAUSAL else Qmf[:, n % 8, :]
                                g.tensor_scalar(dst, src, head_mask[:, n % 8:n % 8 + 1], 1.0, ALU.mult,
                                                ALU.mult).then_inc(mask_done, 1)
                            if what == "pair":
                                pool.wait_ge(t_used, slots[l, "pair", n][1] + 1)
                                for e in range(2):
                                    g.tensor_scalar(Kparts[:, n % 2, e, 0, :], KT[:, e, :], 1.0, 1.0, ALU.mult,
                                                    ALU.mult).then_inc(k_high_done, 1)
                                for e in range(2):
                                    pool.wait_ge(k_high_done, 2 * n + e + 1)
                                    last = g.tensor_tensor(Kparts[:, n % 2, e, 1, :], KT[:, e, :],
                                                           Kparts[:, n % 2, e, 0, :].bitcast(F32), ALU.subtract)
                                last.then_inc(k_parts_done, 1)
                            if what == "norm":
                                h = n
                                pool.wait_ge(rtotal_done, heads_before[l] + h + 1)
                                for q in range(len(widths(layer))):
                                    last = g.tensor_scalar(unit(l, h, q), unit(l, h, q), rtotal[:, h % 8, q:q + 1], 1.0,
                                                           ALU.mult, ALU.mult)
                                last.then_inc(norm_done, 1)

                @block.scalar
                def _(act):
                    a = nc.scalar

                    def full(n):
                        act.wait_ge(t_full, n + 1)

                    def exps(l, h):
                        layer = LAYERS[l]
                        for q in range(len(widths(layer))):
                            slot = slots[l, "scores", h][0 if layer is FFN else q]
                            if layer is BIASED:
                                if q == 0:
                                    act.wait_ge(peak_done, h + 1)
                            elif layer is CAUSAL or q == 0:
                                act.wait_ge(s_used, slot + 1)
                            a.activation(unit(l, h, q), unit(l, h, q), ACT.Exp, bias=peak[:, h % 8, q:q + 1],
                                         scale=1.0 if layer is BIASED else -1.0,
                                         accum_out=total[:, h % 8, q:q + 1]).then_inc(exp_done, 1)

                    for l, layer in enumerate(LAYERS):
                        if layer is not FFN:
                            for c in range(NC):
                                full(slots[l, "xT"][c])
                                a.activation(xnT[:, c, :], t_bank(slots[l, "xT"][c]), ACT.Copy).then_inc(t_used, 1)
                        if layer is CAUSAL:
                            for i in range(NT // 2):
                                n = slots[l, "v"][i]
                                full(n)
                                a.activation(Vpad[:, 2 * i:2 * i + 2, :, 0:DH],
                                             t_bank(n).rearrange("p (t h d) -> p t h d", t=2, h=H),
                                             ACT.Copy).then_inc(t_used, 1)
                            for c in range(4):
                                n = slots[l, "qkT"][c]
                                full(n)
                                a.activation(QTa[:, c, :] if c < 2 else KT[:, c - 2, :], t_bank(n),
                                             ACT.Copy).then_inc(t_used, 1)
                        if layer is FFN:
                            act.wait_ge(logit_done, ffn_no[l] + 1)
                            a.activation(gate[:], z[:], ACT.Exp, scale=-1.0).then_inc(sig_exp_done, 1)
                            n = slots[l, "gather"]
                            full(n)
                            a.activation(xgT, t_bank(n).rearrange("p (c n) -> p c n", c=NC), ACT.Copy).then_inc(t_used, 1)
                            for m in range(2):
                                n = slots[l, "q"][m]
                                full(n)
                                a.activation(QTf[:, m, :], t_bank(n)[:, 0:CAP], ACT.Copy,
                                             scale=-float(DH) ** -0.5).then_inc(t_used, 1)
                            n = slots[l, "k"]
                            full(n)
                            a.activation(KTf, t_bank(n).rearrange("p (c n) -> p c n", c=2), ACT.Copy).then_inc(t_used, 1)
                        for what, n in attention_steps(layer):
                            if what == "pair":
                                _, ks, vs = slots[l, "pair", n]
                                full(ks)
                                if n > 0:
                                    act.wait_ge(k_parts_done, n)
                                for e in range(2):
                                    for half in range(2):
                                        last = a.activation(KT[half * DB:(half + 1) * DB, e, :],
                                                            t_bank(ks)[e * DB:(e + 1) * DB, :], ACT.Copy)
                                last.then_inc(t_used, 1)
                                full(vs)
                                if n >= 4:
                                    act.wait_ge(s_full, slots[l, "values", n - 4] + 1)
                                a.activation(Vb[:, n % 4], t_bank(vs).rearrange("p (t n) -> p t n", t=NT),
                                             ACT.Copy).then_inc(t_used, 1)
                            if what == "scores":
                                exps(l, n)
                            if what == "turn" and any(ring == "t" for ring, _ in slots[l, "turn", n]):
                                old = n - PT_HELD[layer]
                                if old >= 0:
                                    act.wait_ge(s_full, slots[l, "values", old // GROUP[layer]] + 1)
                                for k, (ring, m) in enumerate(slots[l, "turn", n]):
                                    if ring == "t":
                                        full(m)
                                        lo = k * P if layer is CAUSAL else 0
                                        a.activation(pt(l, n, k), t_bank(m)[:, lo:T], ACT.Copy).then_inc(t_used, 1)
                        if layer is FFN:
                            n = slots[l, "o"]
                            full(n)
                            a.activation(of, t_bank(n).rearrange("p (s n) -> p s n", s=NS), ACT.Copy).then_inc(t_used, 1)

                @block.vector
                def _(dve):
                    v = nc.vector

                    def full(n):
                        dve.wait_ge(s_full, n + 1)

                    def layer_norm(l, i):
                        tiles = range(2 * i, 2 * i + 2)
                        k = 2 * l + i + 1
                        src = xin if l == 0 else x
                        if l == 0:
                            dve.wait_ge(x_loaded, it * 16 + 16)
                        else:
                            dve.wait_ge(s_used, slots[l - 1, "y"][i] + 1)
                        for t in tiles:
                            last = v.bn_stats(stats[:, t, :], src[:, t, :])
                        last.then_inc(stats_done, 1)
                        dve.wait_ge(stats_done, k)
                        for t in tiles:
                            last = v.bn_aggr(mv[:, t, :], stats[:, t, :])
                        last.then_inc(mv_done, 1)
                        dve.wait_ge(mv_done, k)
                        v.tensor_scalar(veps[:, 2 * i:2 * i + 2], mv[:, 2 * i:2 * i + 2, 1], EPS, None,
                                        ALU.add).then_inc(veps_done, 1)
                        dve.wait_ge(rstd_done, k)
                        for t in tiles:
                            last = v.tensor_scalar(xn[:, t, :], src[:, t, :], mv[:, t, 0:1], rstd[:, t:t + 1],
                                                   ALU.subtract, ALU.mult)
                        last.then_inc(xn_done, 1)
                        if LAYERS[l] is FFN:
                            dve.wait_ge(xn_done, k)
                            for t in tiles:
                                last = v.tensor_tensor_reduce(out=logit_products[:, t, :], in0=xn[:, t, :], in1=wg[:],
                                                              scale=1.0, scalar=0.0, op0=ALU.mult, op1=ALU.add,
                                                              accum_out=z[:, t:t + 1])
                            if i == 1:
                                last.then_inc(logit_done, 1)

                    for i in range(2):
                        layer_norm(0, i)
                    for l, layer in enumerate(LAYERS):
                        if layer is CAUSAL:
                            for t in range(NT):
                                n = slots[l, "qk"][t]
                                full(n)
                                if t >= 2:
                                    dve.wait_ge(rope_done, t - 1)
                                src = s_bank(n).rearrange("p (a h d) -> p a h d", a=2, h=H)
                                rc = rope_c[:, t % 2, :].rearrange("p (a h d) -> p a h d", a=2, h=H)
                                rs = rope_s[:, t % 2, :].rearrange("p (a h e two) -> p a h e two", a=2, h=H, two=2)
                                sw = s_bank(n).rearrange("p (a h e two) -> p a h e two", a=2, h=H, two=2)
                                st = sin_t[:, t].rearrange("p a (e two) -> p a e two", two=2)
                                for a in range(2):
                                    v.tensor_tensor(rc[:, a], src[:, a],
                                                    cos_t[:, t, a:a + 1, :].to_broadcast([P, H, DH]), ALU.mult)
                                    for odd in range(2):
                                        last = v.tensor_tensor(rs[:, a, :, :, odd], sw[:, a, :, :, 1 - odd],
                                                               st[:, a:a + 1, :, odd].to_broadcast([P, H, DH // 2]),
                                                               ALU.mult)
                                last.then_inc(s_used, 1)

                        if layer is FFN:
                            f = ffn_no[l]
                            dve.wait_ge(sig_exp_done, f + 1)
                            v.tensor_scalar_add(z[:], gate[:], 1.0).then_inc(sig_sum_done, 1)
                            dve.wait_ge(sig_sum_done, f + 1)
                            v.reciprocal(gate[:], z[:]).then_inc(gate_done, 1)
                            n = slots[l, "row"]
                            full(n)
                            v.tensor_copy(gate_row[:], s_bank(n)).then_inc(s_used, 1)
                            dve.wait_ge(s_used, n + 1)
                            for t in range(NT):
                                own = slice(t * P, (t + 1) * P)
                                v.scalar_tensor_tensor(out=tie[:, t, :], in0=gate_row[:, own], scalar=gate[:, t:t + 1],
                                                       in1=before[:], op0=ALU.is_equal, op1=ALU.mult)
                            for t in range(NT):
                                last = v.tensor_scalar(above[:, t, 0:(t + 1) * P], gate_row[:, 0:(t + 1) * P],
                                                       gate[:, t:t + 1], None, ALU.is_lt)
                                if t < NT - 1:
                                    v.tensor_scalar(above[:, t, (t + 1) * P:T], gate_row[:, (t + 1) * P:T],
                                                    gate[:, t:t + 1], None, ALU.is_le)
                            last.then_inc(above_done, 1)
                            cn, rn = slots[l, "rank"]
                            full(cn)
                            v.tensor_copy(rank[:], s_bank(cn)[:, 0:NT]).then_inc(s_used, 1)
                            dve.wait_ge(s_used, cn + 1)
                            for t in range(NT):
                                last = v.tensor_scalar(pick[:, t, :], slot_row[:], rank[:, t:t + 1], None, ALU.is_equal)
                            last.then_inc(pick_done, 1)
                            full(rn)
                            for s in range(NS):
                                last = v.scalar_tensor_tensor(out=spread[:, s, :], in0=s_bank(rn),
                                                              scalar=slot_col[:, s:s + 1], in1=gate_row[:],
                                                              op0=ALU.is_equal, op1=ALU.mult)
                            last.then_inc(s_used, 1)
                            n = slots[l, "v"]
                            full(n)
                            v.tensor_copy(Vpad[:, 0:NS, :, 0:DH],
                                          s_bank(n).rearrange("p (t h d) -> p t h d", t=NS, h=H)).then_inc(s_used, 1)

                        def inverse(h):
                            dve.wait_ge(exp_done, units_before[l] + (h + 1) * len(widths(layer)))
                            w = len(widths(layer))
                            v.reciprocal(rtotal[:, h % 8, 0:w], total[:, h % 8, 0:w]).then_inc(rtotal_done, 1)

                        for what, n in attention_steps(layer):
                            if what == "pair":
                                m = slots[l, "pair", n][0]
                                full(m)
                                for e in range(2):
                                    rows = slice(e * DB, (e + 1) * DB)
                                    v.tensor_scalar(Qparts[rows, (2 * n + e) % 4, :], s_bank(m)[rows, :], float(DB) ** -0.5,
                                                    None, ALU.mult).then_inc(q_high_done, 1)
                                for e in range(2):
                                    rows, others = slice(e * DB, (e + 1) * DB), slice((1 - e) * DB, (2 - e) * DB)
                                    dve.wait_ge(q_high_done, 2 * n + e + 1)
                                    last = v.scalar_tensor_tensor(out=Qparts[others, (2 * n + e) % 4, :],
                                                                  in0=s_bank(m)[rows, :], scalar=float(DB) ** -0.5,
                                                                  in1=Qparts[rows, (2 * n + e) % 4, :].bitcast(F32),
                                                                  op0=ALU.mult, op1=ALU.subtract)
                                last.then_inc(s_used, 1)
                            if what == "scores":
                                if n >= HELD[layer]:
                                    ring, m = slots[l, "turn", n - HELD[layer]][-1]
                                    dve.wait_ge(s_full if ring == "s" else t_full, m + 1)
                                if layer is BIASED:
                                    dve.wait_ge(band_loaded[n % BANDS], 16 * (n // BANDS + 1))
                                for q, w in enumerate(widths(layer)):
                                    m = slots[l, "scores", n][0 if layer is FFN else q]
                                    if layer is not FFN or q == 0:
                                        dve.wait_ge(s_full, m + 1)
                                    if layer is FFN:
                                        src, add = s_bank(m)[:, q * CAP:(q + 1) * CAP], hide[:, 0:CAP]
                                    elif layer is CAUSAL:
                                        src, add = s_bank(m)[:, 0:w], hide[:, T - w:T]
                                    else:
                                        lo = (NT - 1 - q) * P
                                        src, add = s_bank(m), band[:, n % BANDS, lo:lo + T]
                                    sign = 1 if layer is BIASED else -1
                                    last = v.tensor_tensor_reduce(out=unit(l, n, q), in0=src, in1=add, scale=1.0,
                                                                  scalar=-sign * 3e38, op0=ALU.add,
                                                                  op1=ALU.max if layer is BIASED else ALU.min,
                                                                  accum_out=peak[:, n % 8, q:q + 1])
                                    if layer is not FFN or q == NS - 1:
                                        last.then_inc(s_used, 1)
                                if layer is BIASED:
                                    dve.wait_ge(s_used, slots[l, "scores", n][-1] + 1)
                                    v.tensor_scalar(peak[:, n % 8, :], peak[:, n % 8, :], -1.0, None,
                                                    ALU.mult).then_inc(peak_done, 1)
                            if what == "norm":
                                inverse(n)
                            if what == "turn" and any(ring == "s" for ring, _ in slots[l, "turn", n]):
                                old = n - PT_HELD[layer]
                                if old >= 0:
                                    dve.wait_ge(s_full, slots[l, "values", old // GROUP[layer]] + 1)
                                for k, (ring, m) in enumerate(slots[l, "turn", n]):
                                    if ring == "s":
                                        full(m)
                                        if layer is FFN:
                                            o = (n % PT_HELD[layer]) * NS * CAP
                                            dst = PT[:, o:o + NS * CAP]
                                        else:
                                            dst = pt(l, n, k)
                                        lo = k * P if layer is CAUSAL else 0
                                        v.tensor_copy(dst, s_bank(m)[:, lo:T]).then_inc(s_used, 1)
                            if what == "values":
                                m = slots[l, "values", n]
                                full(m)
                                dst = {CAUSAL: OTa, BIASED: OTb, FFN: OTf}[layer][:, n, :]
                                v.tensor_copy(dst, s_bank(m)[:, 0:CAP if layer is FFN else T]).then_inc(s_used, 1)

                        for i in range(NT // 2):
                            n = slots[l, "y"][i]
                            full(n)
                            if l == 0:
                                dve.wait_ge(x_stored, it * 16 + 16)
                            last = v.tensor_tensor(x[:, 2 * i:2 * i + 2, :], (xin if l == 0 else x)[:, 2 * i:2 * i + 2, :],
                                                   s_bank(n).rearrange("p (t d) -> p t d", t=2), ALU.add)
                            last.then_inc(s_used, 1)
                            if l < NL - 1:
                                layer_norm(l + 1, i)
                    dve.wait_ge(s_used, slots[NL - 1, "y"][-1] + 1)
                    dve.sem_inc(x_done, 1)

                @block.tensor
                def _(pe):
                    te = nc.tensor

                    def s_slot(n):
                        if n >= SB:
                            pe.wait_ge(s_used, n - SB + 1)
                        return s_bank(n)

                    def t_slot(n):
                        if n >= SB:
                            pe.wait_ge(t_used, n - SB + 1)
                        return t_bank(n)

                    def s_ready(n):
                        pe.wait_ge(s_used, n + 1)

                    def t_ready(n):
                        pe.wait_ge(t_used, n + 1)

                    def product(o, pairs):
                        for i, (w, r) in enumerate(pairs):
                            last = te.matmul(o, w, r, start=(i == 0), stop=(i == len(pairs) - 1))
                        return last

                    for l, layer in enumerate(LAYERS):
                        if layer is not FFN:
                            for i in range(2):
                                pe.wait_ge(xn_done, 2 * l + i + 1)
                                for c in range(NC):
                                    n = slots[l, "xT"][c]
                                    o = t_slot(n) if i == 0 else t_bank(n)
                                    for t in range(2 * i, 2 * i + 2):
                                        last = te.transpose(o[:, t * P:(t + 1) * P], xn[:, t, c * P:(c + 1) * P], ident[:])
                                    if i == 1:
                                        last.then_inc(t_full, 1)
                            t_ready(slots[l, "xT"][-1])
                        if layer is CAUSAL:
                            for t in range(NT):
                                o = s_slot(slots[l, "qk"][t])
                                product(o, [(xnT[:, c, t * P:(t + 1) * P], wqk[:, c, :])
                                            for c in range(NC)]).then_inc(s_full, 1)
                            for i in range(NT // 2):
                                o = t_slot(slots[l, "v"][i])
                                for j in range(2):
                                    t = 2 * i + j
                                    last = product(o[:, j * D:(j + 1) * D],
                                                   [(xnT[:, c, t * P:(t + 1) * P], wva[:, c, :]) for c in range(NC)])
                                last.then_inc(t_full, 1)
                            for c in range(4):
                                o = t_slot(slots[l, "qkT"][c])
                                for t in range(NT):
                                    if c == 0:
                                        pe.wait_ge(rope_done, t + 1)
                                    last = te.transpose(o[:, t * P:(t + 1) * P], qkr[:, t, c * P:(c + 1) * P], ident[:])
                                last.then_inc(t_full, 1)
                            t_ready(slots[l, "qkT"][-1])
                        if layer is FFN:
                            f = ffn_no[l]
                            pe.wait_ge(gate_done, f + 1)
                            o = s_slot(slots[l, "row"])
                            for t in range(NT):
                                last = te.transpose(o[:, t * P:(t + 1) * P], gate[:, t:t + 1].to_broadcast([P, P]), ident[:])
                            last.then_inc(s_full, 1)
                            pe.wait_ge(above_done, f + 1)
                            cn, rn = slots[l, "rank"]
                            o = s_slot(cn)
                            for i in range(NT):
                                own = slice(i * P, (i + 1) * P)
                                last = product(o[:, i:i + 1], [(tie[:, i, :], ones[:, 0:1])] +
                                               [(above[:, t, own], ones[:, 0:1]) for t in range(NT)])
                            last.then_inc(s_full, 1)
                            o = s_slot(rn)
                            for t in range(NT):
                                last = te.matmul(o, ones[:], above[:, t, :], start=(t == 0), stop=(t == NT - 1))
                                if t == 0:
                                    for i in range(NT):
                                        te.matmul(o[:, i * P:(i + 1) * P], ones[:], tie[:, i, :], start=False, stop=False)
                            last.then_inc(s_full, 1)
                            pe.wait_ge(pick_done, f + 1)
                            o = t_slot(slots[l, "gather"])
                            for c in range(NC):
                                last = product(o[:, c * CAP:(c + 1) * CAP], [(xn[:, t, c * P:(c + 1) * P], pick[:, t, :])
                                                                             for t in range(NT)])
                            last.then_inc(t_full, 1)
                            t_ready(slots[l, "gather"])
                            for m in range(2):
                                product(t_slot(slots[l, "q"][m])[:, 0:CAP],
                                        [(wqf[:, c, m * P:(m + 1) * P], xgT[:, c, :]) for c in range(NC)]).then_inc(t_full, 1)
                            o = t_slot(slots[l, "k"])
                            for m in range(2):
                                last = product(o[:, m * CAP:(m + 1) * CAP],
                                               [(wkf[:, c, m * P:(m + 1) * P], xgT[:, c, :]) for c in range(NC)])
                            last.then_inc(t_full, 1)
                            o = s_slot(slots[l, "v"])
                            for s in range(NS):
                                last = product(o[:, s * D:(s + 1) * D],
                                               [(xgT[:, c, s * P:(s + 1) * P], wvf[:, c, :]) for c in range(NC)])
                            last.then_inc(s_full, 1)
                            t_ready(slots[l, "k"])
                            s_ready(slots[l, "v"])

                        for what, n in attention_steps(layer):
                            if what == "pair":
                                if n == 0:
                                    pe.wait_ge(w_late, W_LATE)
                                qs, ks, vs = slots[l, "pair", n]
                                product(s_slot(qs), [(wb[:, c, 0, n * P:(n + 1) * P], xnT[:, c, :])
                                                     for c in range(NC)]).then_inc(s_full, 1)
                                product(t_slot(ks), [(wb[:, c, 1, n * P:(n + 1) * P], xnT[:, c, :])
                                                     for c in range(NC)]).then_inc(t_full, 1)
                                o = t_slot(vs)
                                for t in range(NT):
                                    last = product(o[:, t * P:(t + 1) * P],
                                                   [(xnT[:, c, t * P:(t + 1) * P], wb[:, c, 2, n * P:(n + 1) * P])
                                                    for c in range(NC)])
                                last.then_inc(t_full, 1)
                            if what == "scores":
                                if layer is BIASED:
                                    s_ready(slots[l, "pair", n // 2][0])
                                    pe.wait_ge(k_parts_done, n // 2 + 1)
                                else:
                                    pe.wait_ge(mask_done, mask_before[l] + n + 1)
                                    keys = KT[:, n // 8, :] if layer is CAUSAL else KTf[:, n // 8, :]
                                for q, w in enumerate(widths(layer)):
                                    m = slots[l, "scores", n][0 if layer is FFN else q]
                                    if layer is FFN:
                                        o = (s_slot(m) if q == 0 else s_bank(m))[:, q * CAP:(q + 1) * CAP]
                                    else:
                                        o = s_slot(m)[:, 0:w]
                                    rows = slice(q * P, (q + 1) * P)
                                    if layer is BIASED:
                                        last = product(o, [(Qparts[:, n % 4, rows], Kparts[:, (n // 2) % 2, n % 2, part, :])
                                                           for part in range(2)])
                                    else:
                                        qs = Qmf[:, n % 8, :] if layer is FFN else Qm[:, n % 4, :]
                                        last = te.matmul(o, qs[:, rows], keys[:, 0:w], start=True, stop=True)
                                    if layer is not FFN or q == NS - 1:
                                        last.then_inc(s_full, 1)
                            if what == "turn":
                                pe.wait_ge(norm_done, heads_before[l] + n + 1)
                                for k, (ring, m) in enumerate(slots[l, "turn", n]):
                                    o = s_slot(m) if ring == "s" else t_slot(m)
                                    if layer is FFN:
                                        blocks = [(q, i) for i in range(NS) for q in range(NS)]
                                    else:
                                        blocks = [(q, k) for q in range(k if layer is CAUSAL else 0, NT)]
                                    for q, i in blocks:
                                        at = (i * CAP if layer is FFN else 0) + q * P
                                        last = te.transpose(o[:, at:at + P], unit(l, n, q)[:, i * P:(i + 1) * P],
                                                            ident[:])
                                    last.then_inc(s_full if ring == "s" else t_full, 1)
                            if what == "values":
                                size = GROUP[layer]
                                heads = range(size * n, size * n + size)
                                for ring in "st":
                                    m = [m for r, m in slots[l, "turn", heads[-1]] if r == ring]
                                    if m:
                                        (s_ready if ring == "s" else t_ready)(m[-1])
                                m = slots[l, "values", n]
                                o = s_slot(m)
                                if layer is BIASED:
                                    t_ready(slots[l, "pair", n][2])
                                rows = P // size
                                for k in range(NS if layer is FFN else NT):
                                    for e, h in enumerate(heads):
                                        lo = k * P if layer is CAUSAL else 0
                                        hi = CAP if layer is FFN else T
                                        w = Vb[:, n % 4, k, e * DB:(e + 1) * DB] if layer is BIASED else Vpad[:, k, h, :]
                                        last = te.matmul(o[e * rows:(e + 1) * rows, lo:hi], w, pt(l, h, k), start=(k == 0),
                                                         stop=(k == (NS if layer is FFN else NT) - 1))
                                last.then_inc(s_full, 1)

                        s_ready(slots[l, "values", H // GROUP[layer] - 1])
                        if layer is FFN:
                            o = t_slot(slots[l, "o"])
                            for s in range(NS):
                                last = product(o[:, s * D:(s + 1) * D],
                                               [(OTf[:, g, s * P:(s + 1) * P], wof[:, g, :]) for g in range(NG)])
                            last.then_inc(t_full, 1)
                            t_ready(slots[l, "o"])
                        for i in range(NT // 2):
                            o = s_slot(slots[l, "y"][i])
                            for j in range(2):
                                cols = slice((2 * i + j) * P, (2 * i + j + 1) * P)
                                if layer is FFN:
                                    pairs = [(spread[:, s, cols], of[:, s, :]) for s in range(NS)]
                                elif layer is CAUSAL:
                                    pairs = [(OTa[:, g, cols], woa[:, g, :]) for g in range(NG)]
                                else:
                                    pairs = [(OTb[:, m, cols], wob[:, m, :]) for m in range(H * DB // P)]
                                last = product(o[:, j * D:(j + 1) * D], pairs)
                            last.then_inc(s_full, 1)


            nc.all_engine_barrier(sems_to_clear=batch_sems)
        with nc.Block() as end:

            @end.sync
            def _(sp):
                sp.wait_ge(x_stored, 16 * (B + 1))
                sp.wait_ge(x_loaded, 16 * (B + 1))


def kernel(L0_attn_a_x, L0_attn_a_Wq, L0_attn_a_Wk, L0_attn_a_Wv, L0_attn_a_Wo, L0_attn_b_w_qkv, L0_attn_b_w_out,
           L0_attn_b_rel_bias, L0_ffn_Wg, L0_ffn_Wq, L0_ffn_Wk, L0_ffn_Wv, L0_ffn_Wo):
    import numpy as np
    import concourse.bacc as bacc
    from concourse.bass_utils import run_bass_kernel_spmd

    def chunks(w):
        w = np.asarray(w)
        return np.ascontiguousarray(w.reshape(-1, P, w.shape[-1]).transpose(1, 0, 2))

    def gapped(w):
        w = np.asarray(w)
        g = np.zeros((H, GAP, D), w.dtype)
        g[:, :DH] = w.reshape(H, DH, D)
        return chunks(g.reshape(H * GAP, D))

    inv = np.float32(10000.0) ** (-(np.arange(DH // 2, dtype=np.float32) * np.float32(2.0 / DH)))
    angle = np.arange(T, dtype=np.float32)[:, None] * inv[None, :].astype(np.float32)
    cos = np.repeat(np.cos(angle), 2, axis=1).astype(np.float32)
    sin = np.stack([-np.sin(angle), np.sin(angle)], axis=-1).reshape(T, DH).astype(np.float32)
    scale = np.array([-float(DH) ** -0.5, 1.0], np.float32)[None, :, None]
    cos2 = np.ascontiguousarray((cos[:, None, :] * scale).reshape(NT, P, 2, DH).transpose(1, 0, 2, 3))
    sin2 = np.ascontiguousarray((sin[:, None, :] * scale).reshape(NT, P, 2, DH).transpose(1, 0, 2, 3))
    head_mask = (np.arange(P)[:, None] // DH == np.arange(8)[None, :]).astype(np.float32)
    at = np.minimum(np.arange(BAND)[None, :] - np.arange(P)[:, None] + P - 1, REL - 1)
    band = np.ascontiguousarray(np.asarray(L0_attn_b_rel_bias).T[:, at])

    w_b = np.asarray(L0_attn_b_w_qkv).reshape(DB, 3, H, D).transpose(3, 1, 2, 0).reshape(D, 3 * H * DB)
    w_b = chunks(w_b).reshape(P, NC, 3, H * DB)
    wqk_a = chunks(np.concatenate([np.asarray(L0_attn_a_Wq).T, np.asarray(L0_attn_a_Wk).T], axis=1))
    arrays = {
        "x": np.asarray(L0_attn_a_x),
        "wqk_a": wqk_a,
        "wv_a": chunks(np.asarray(L0_attn_a_Wv).T),
        "wo_a": gapped(np.asarray(L0_attn_a_Wo).T),
        "w_b": w_b,
        "wo_b": chunks(np.asarray(L0_attn_b_w_out).T),
        "band": band,
        "wg_f": np.ascontiguousarray(np.broadcast_to(np.asarray(L0_ffn_Wg).reshape(1, D), (P, D))),
        "wq_f": chunks(L0_ffn_Wq),
        "wk_f": chunks(L0_ffn_Wk),
        "wv_f": chunks(L0_ffn_Wv),
        "wo_f": gapped(L0_ffn_Wo),
        "cos": cos2,
        "sin": sin2,
        "head_mask": head_mask,
    }
    nc = bacc.Bacc("TRN2", target_bir_lowering=False, num_devices=1)
    ins = {f"in_{k}": np.ascontiguousarray(a) for k, a in arrays.items()}
    aps = [nc.dram_tensor(k, a.shape, mybir.dt.from_np(a.dtype), kind="ExternalInput").ap() for k, a in ins.items()]
    out = nc.dram_tensor("out", (B, T, D), F32, kind="ExternalOutput").ap()
    hybrid_kernel(nc, *aps, out)
    r = run_bass_kernel_spmd(nc, [ins], core_ids=[0])
    return r.results[0]["out"]
```

```python
from contextlib import ExitStack

import concourse.bass as bass
from concourse import mybir

F32 = mybir.dt.float32
F32R = mybir.dt.float32r
BF16 = mybir.dt.bfloat16
ALU = mybir.AluOpType
ACT = mybir.ActivationFunctionType

P = 128
B, T, D = 8, 512, 256
NT, NC = T // P, D // P
H = 16
DH = D // H
DB = 64
CAP = T // 2
NS = CAP // P
GAP = 32
VROW = 2 * (H // 2 * GAP + DH)
REL = 2 * 256 - 1
BAND = T + (NT - 1) * P
BANDS = 3
EPS = 1e-5
FAR = 1e30
SB = 4

CAUSAL, BIASED, FFN = "causal", "biased", "ffn"
LAYERS = (CAUSAL, FFN, BIASED, FFN)


class Ring:

    def __init__(self):
        self.n = 0

    def take(self):
        self.n += 1
        return self.n - 1


HELD = {CAUSAL: 4, BIASED: 3, FFN: 8}
AHEAD = {CAUSAL: 3, BIASED: 3, FFN: 5}
MASK_AHEAD = {CAUSAL: 2, FFN: 3}
NORM_LAG = {CAUSAL: 1, BIASED: 1, FFN: 2}
PT_HELD = {CAUSAL: 5, BIASED: 3, FFN: 6}
Q_HELD = {CAUSAL: 4, BIASED: 4, FFN: 8}
GROUP = {CAUSAL: 4, BIASED: 2, FFN: 4}


TURN_FIRST = (BIASED,)
SCALAR_TURNS = (13, 15)
WARM = {"input": 3, "gates": 6, "ranks": 4}
SCALAR_NORMS = {CAUSAL: (), BIASED: (), FFN: (12, 14)}
NEXT_TURNS = (3, 5, 7, 9)


def layer_steps(l):
    for what, n in attention_steps(LAYERS[l]):
        yield what, n
        if l == len(LAYERS) - 1 and what == "scores" and n in NEXT_TURNS:
            yield "next_turn", NEXT_TURNS.index(n)


def attention_steps(layer):
    out = []
    ahead, lag, group = AHEAD[layer], NORM_LAG[layer], GROUP[layer]
    for n in range(H + ahead + 1):
        if layer is BIASED:
            if n == 0:
                out.append(("pair", 0))
            if n % 2 == 0 and n + 2 < H:
                out.append(("pair", n // 2 + 1))
        else:
            more = MASK_AHEAD[layer]
            for m in range(more + 1) if n == 0 else range(n + more, n + more + 1):
                if m < H:
                    out.append(("mask", m))
        h = n - ahead
        if 0 <= h < H and layer in TURN_FIRST:
            out.append(("turn", h))
        if n < H:
            out.append(("scores", n))
        if 0 <= n - lag < H:
            out.append(("norm", n - lag))
        if 0 <= h < H and layer not in TURN_FIRST:
            out.append(("turn", h))
        if h >= 1 and h % group == 0:
            out.append(("values", h // group - 1))
    return out


def hybrid_kernel(nc, x_in, wqk_a, wv_a, wo_a, w_b, wo_b, band_in, wg_f, wq_f, wk_f, wv_f, wo_f,
                  cos_in, sin_in, head_mask_in, out):
    with ExitStack() as ctx:
        def sb(name, shape, dt=F32):
            return ctx.enter_context(nc.sbuf_tensor(name, shape, dt))

        def sem(name):
            return ctx.enter_context(nc.semaphore(name))

        wqk = sb("wqk", [P, NC, 2 * D])
        wva = sb("wva", [P, NC, D])
        woa = sb("woa", [P, NC, D])
        wb = sb("wb", [P, NC, 3, H * DB])
        wob = sb("wob", [P, H * DB // P, D])
        wg = sb("wg", [P, D])
        wqf = sb("wqf", [P, NC, D])
        wkf = sb("wkf", [P, NC, D])
        wvf = sb("wvf", [P, NC, D])
        wof = sb("wof", [P, NC, D])
        cos_t = sb("cos_t", [P, NT, 2, DH])
        sin_t = sb("sin_t", [P, NT, 2, DH])
        head_mask = sb("head_mask", [P, 8])
        ident = sb("ident", [P, P])
        hide = sb("hide", [P, T])
        before = sb("before", [P, P], BF16)
        ones = sb("ones", [P, P], BF16)
        slot_row = sb("slot_row", [P, CAP])
        slot_col = sb("slot_col", [P, NS])

        xin = sb("xin", [P, NT, D])
        x = sb("x", [P, NT, D])
        xn = sb("xn", [P, NT, D])
        xnT = sb("xnT", [P, NC, T])
        stats = sb("stats", [P, NT, 6])
        mv = sb("mv", [P, NT, 2])
        veps = sb("veps", [P, NT])
        rstd = sb("rstd", [P, NT])
        pow_half = sb("pow_half", [P, NT])
        work = sb("work", [P, 8 * T])
        QTa = sb("QTa", [P, 2, T])
        KTa = sb("KTa", [P, 2, T])
        QTf = sb("QTf", [P, 2, CAP])
        Qparts = sb("Qparts", [P, 4, T], F32R)
        Kparts = sb("Kparts", [P, 2, 2, 2, T], F32R)
        Vb = sb("Vb", [P, 4, NT, P])
        band = sb("band", [P, BANDS, BAND])
        Vpad = sb("Vpad", [P, NT, VROW])
        Vf = sb("Vf", [P, NS, VROW])
        probs = sb("probs", [P, 12 * T])
        PT = sb("PT", [P, 5 * 10 * P])
        peak = sb("peak", [P, 8, NT])
        total = sb("total", [P, 8, NT])
        rtotal = sb("rtotal", [P, 8, NT])
        z = sb("z", [P, NT])
        gate = sb("gate", [P, NT])
        gate_row = sb("gate_row", [P, T])
        rank = sb("rank", [P, NT])
        tie = sb("tie", [P, NT, P], BF16)
        logit_products = probs[:, 0:2 * T].rearrange("p (t d) -> p t d", d=D)
        xn_next = PT[:, 6 * T:8 * T].rearrange("p (t d) -> p t d", d=D)
        qk_next = PT[:, 8 * T:12 * T].rearrange("p (t n) -> p t n", t=NT)
        partner = probs[:, 8 * T:12 * T].rearrange("p (t n) -> p t n", t=NT)

        OTa = work[:, 0:NC * T].rearrange("p (g n) -> p g n", g=NC)
        OTb = work[:, :].rearrange("p (m n) -> p m n", m=8)
        OTf = work[:, 0:NC * CAP].rearrange("p (g n) -> p g n", g=NC)
        spread = work[:, 2 * T:4 * T].rearrange("p (s n) -> p s n", s=NS)
        pick = work[:, 4 * T:6 * T].rearrange("p (t n) -> p t n", t=NT)
        above = work[:, 6 * T:8 * T].bitcast(BF16).rearrange("p (t n) -> p t n", t=NT)
        of = work[:, 6 * T:7 * T].rearrange("p (s n) -> p s n", s=NS)
        xgT = work[:, 4 * T:5 * T].rearrange("p (c n) -> p c n", c=NC)
        Qm = Vb[:, :, :, :].rearrange("p r t n -> p r (t n)")
        KT = xn[:, :, :].rearrange("p (c t) d -> p c (t d)", c=2)
        Qmf = Vb[:, :, :, :].rearrange("p r (e u) n -> p (r e) (u n)", e=2)
        KTf = KT[:, 0, :].rearrange("p (c n) -> p c n", c=2)

        ps_s = ctx.enter_context(nc.psum_tensor("ps_s", [P, SB, T], F32))
        ps_t = ctx.enter_context(nc.psum_tensor("ps_t", [P, SB, T], F32))

        w_early = sem("w_early")
        w_late = sem("w_late")
        consts = sem("consts")
        const_step = sem("const_step")
        x_loaded = sem("x_loaded")
        x_stored = sem("x_stored")
        s_full = sem("s_full")
        s_used = sem("s_used")
        t_full = sem("t_full")
        t_used = sem("t_used")
        stats_done = sem("stats_done")
        mv_done = sem("mv_done")
        veps_done = sem("veps_done")
        rstd_done = sem("rstd_done")
        xn_done = sem("xn_done")
        x_done = sem("x_done")
        swap_done = sem("swap_done")
        partner_done = sem("partner_done")
        rope_done = sem("rope_done")
        mask_done = sem("mask_done")
        peak_done = sem("peak_done")
        exp_done = sem("exp_done")
        rtotal_done = sem("rtotal_done")
        norm_done = sem("norm_done")
        scalar_norm_done = sem("scalar_norm_done")
        logit_done = sem("logit_done")
        sig_exp_done = sem("sig_exp_done")
        sig_sum_done = sem("sig_sum_done")
        gate_done = sem("gate_done")
        row_done = sem("row_done")
        above_done = sem("above_done")
        rank_done = sem("rank_done")
        pick_done = sem("pick_done")
        q_high_done = sem("q_high_done")
        k_high_done = sem("k_high_done")
        k_parts_done = sem("k_parts_done")
        band_loaded = [sem(f"band_loaded{i}") for i in range(BANDS)]
        batch_sems = range(s_full.num, band_loaded[-1].num + 1)

        NL = len(LAYERS)
        NHEADS = NL * H
        heads_before = [l * H for l in range(NL)]
        W_EARLY, W_LATE, CONSTS = 11 * 16, 2 * 16, 10

        def turned_by_vector(layer, h, k):
            return layer is FFN and h not in SCALAR_TURNS or layer is CAUSAL and k < 2

        s_ring, t_ring = Ring(), Ring()
        slots = {}
        for l, layer in enumerate(LAYERS):
            if layer is BIASED:
                slots[l, "xT"] = [t_ring.take() for _ in range(NC)]
            if l == NL - 1:
                slots["next", "xT"] = [t_ring.take() for _ in range(NC)]
                slots["next", "qk"] = [t_ring.take() for _ in range(NT)]
                slots["next", "v"] = [t_ring.take()]
            if layer is FFN:
                slots[l, "row"] = s_ring.take()
                slots[l, "rank"] = [s_ring.take() for _ in range(2)]
                slots[l, "gather"] = t_ring.take()
                if l == NL - 1:
                    slots["next", "v"].append(t_ring.take())
                slots[l, "q"] = t_ring.take(), t_ring.take()
                slots[l, "k"] = t_ring.take()
                slots[l, "v"] = s_ring.take()
            for what, n in layer_steps(l):
                if what == "next_turn":
                    slots["next", "qkT", n] = t_ring.take()
                if what == "pair":
                    slots[l, "pair", n] = s_ring.take(), t_ring.take(), t_ring.take()
                if what == "scores":
                    slots[l, "scores", n] = [s_ring.take() for _ in range(1 if layer is FFN else NT)]
                if what == "turn":
                    slots[l, "turn", n] = [("s", s_ring.take()) if turned_by_vector(layer, n, k) else ("t", t_ring.take())
                                           for k in range(1 if layer is FFN else NT)]
                if what == "values":
                    slots[l, "values", n] = s_ring.take()
            if layer is FFN:
                slots[l, "o"] = t_ring.take()
            slots[l, "y"] = [s_ring.take() for _ in range(NT // 2)]
        NSS, NTS = s_ring.n, t_ring.n
        assert NSS % SB == 0 and NTS % SB == 0, (NSS, NTS)

        ahead_ring = Ring()
        slots["first", "xT"] = [ahead_ring.take() for _ in range(NC)]
        slots["first", "qk"] = [ahead_ring.take() for _ in range(NT)]
        slots["first", "v"] = [ahead_ring.take() for _ in range(NT // 2)]
        for c in range(4):
            slots["first", "qkT", c] = ahead_ring.take()
        norm_no = {"first": 0, 1: 0, 2: 1, "next": 2, 3: 3}

        def v_places(dst, t):
            return dst[:, t, :].rearrange("p (o j d) -> p o j d", o=2, d=DH)[:, :, 0:H:2, :]

        def v_heads(src):
            return src.rearrange("p (o j d) -> p o j d", o=2, d=DH)

        def v_head(src, t, h):
            group = h // 4
            at = (group % 2 * (H // 2) + group // 2 * 4 + h % 4) * GAP
            return src[:, t, at:at + GAP]

        def s_bank(n):
            return ps_s[:, n % SB, :]

        def t_bank(n):
            return ps_t[:, n % SB, :]

        def widths(layer):
            return {CAUSAL: [P * (q + 1) for q in range(NT)], BIASED: [T] * NT, FFN: [CAP] * NS}[layer]

        units_before = []
        n_units = 0
        for layer in LAYERS:
            units_before.append(n_units)
            n_units += H * len(widths(layer))

        def unit(l, h, q):
            w = widths(LAYERS[l])
            o = (h % HELD[LAYERS[l]]) * sum(w) + sum(w[:q])
            return probs[:, o:o + w[q]]

        def pt(l, h, k):
            layer = LAYERS[l]
            if layer is FFN:
                o = (h % PT_HELD[layer]) * NS * CAP + k * CAP
                return PT[:, o:o + CAP]
            if layer is BIASED:
                o = (h % PT_HELD[layer]) * NT * T + k * T
                return PT[:, o:o + T]
            starts = [0, 4 * P, 7 * P, 9 * P, 10 * P]
            o = (h % PT_HELD[layer]) * starts[-1] + starts[k]
            return PT[:, o:o + starts[k + 1] - starts[k]]

        def turned(l, h, k):
            if LAYERS[l] is FFN:
                o = (h % PT_HELD[FFN]) * NS * CAP
                return PT[:, o:o + NS * CAP]
            return pt(l, h, k)

        norms = {}
        counts = {True: 0, False: 0}
        for l, layer in enumerate(LAYERS):
            for h in range(H):
                by_scalar = h in SCALAR_NORMS[layer]
                counts[by_scalar] += 1
                norms[l, h] = by_scalar, counts[by_scalar]

        mask_before = {l: sum(H for k in range(l) if LAYERS[k] is not BIASED) for l in range(NL)}
        NMASK = sum(H for k in LAYERS if k is not BIASED)
        ffn_no = {l: sum(1 for k in range(l) if LAYERS[k] is FFN) for l in range(NL)}
        NF = 2

        xv = x_in.rearrange("b (t p) d -> b p t d", p=P)
        ov = out.rearrange("b (t p) d -> b p t d", p=P)
        def s_slot(n):
            if n >= SB:
                nc.tensor.wait_ge(s_used, n - SB + 1)
            return s_bank(n)

        def t_slot(n):
            if n >= SB:
                nc.tensor.wait_ge(t_used, n - SB + 1)
            return t_bank(n)

        def product(o, pairs):
            for i, (w, r) in enumerate(pairs):
                last = nc.tensor.matmul(o, w, r, start=(i == 0), stop=(i == len(pairs) - 1))
            return last

        def moments(dve, which, src, i):
            v = nc.vector
            tiles = range(2 * i, 2 * i + 2)
            k = 2 * norm_no[which] + i + 1
            for t in tiles:
                last = v.bn_stats(stats[:, t, :], src[:, t, :])
            last.then_inc(stats_done, 1)
            dve.wait_ge(stats_done, k)
            for t in tiles:
                last = v.bn_aggr(mv[:, t, :], stats[:, t, :])
            last.then_inc(mv_done, 1)
            dve.wait_ge(mv_done, k)
            v.tensor_scalar(veps[:, 2 * i:2 * i + 2], mv[:, 2 * i:2 * i + 2, 1], EPS, None,
                            ALU.add).then_inc(veps_done, 1)

        def normalise(dve, which, src, dst, i):
            v = nc.vector
            tiles = range(2 * i, 2 * i + 2)
            k = 2 * norm_no[which] + i + 1
            dve.wait_ge(rstd_done, k)
            for t in tiles:
                last = v.tensor_scalar(dst[:, t, :], src[:, t, :], mv[:, t, 0:1], rstd[:, t:t + 1],
                                       ALU.subtract, ALU.mult)
            last.then_inc(xn_done, 1)

        def inverse_deviations(pool, which):
            for i in range(2):
                pool.wait_ge(veps_done, 2 * norm_no[which] + i + 1)
                nc.gpsimd.tensor_tensor(rstd[:, 2 * i:2 * i + 2], veps[:, 2 * i:2 * i + 2], pow_half[:, 0:2],
                                        ALU.pow).then_inc(rstd_done, 1)

        def transpose_input(pe, which, key, src):
            for i in range(2):
                pe.wait_ge(xn_done, 2 * norm_no[which] + i + 1)
                for c in range(NC):
                    n = slots[key, "xT"][c]
                    o = t_slot(n) if i == 0 else t_bank(n)
                    for t in range(2 * i, 2 * i + 2):
                        last = nc.tensor.transpose(o[:, t * P:(t + 1) * P], src[:, t, c * P:(c + 1) * P], ident[:])
                    if i == 1:
                        last.then_inc(t_full, 1)

        def move_input(act, key):
            for c in range(NC):
                act.wait_ge(t_full, slots[key, "xT"][c] + 1)
                nc.scalar.activation(xnT[:, c, :], t_bank(slots[key, "xT"][c]), ACT.Copy).then_inc(t_used, 1)

        def project_qk(pe, which, tiles):
            pe.wait_ge(t_used, slots[which, "xT"][-1] + 1)
            for t in tiles:
                product(t_slot(slots[which, "qk"][t]), [(xnT[:, c, t * P:(t + 1) * P], wqk[:, c, :])
                                                        for c in range(NC)]).then_inc(t_full, 1)

        def move_qk(act, which, tiles):
            for t in tiles:
                n = slots[which, "qk"][t]
                act.wait_ge(t_full, n + 1)
                nc.scalar.activation(qk_next[:, t, :], t_bank(n), ACT.Copy).then_inc(t_used, 1)

        def rotate(dve, which):
            v = nc.vector
            for t in range(NT):
                dve.wait_ge(t_used, slots[which, "qk"][t] + 1)
                sw = qk_next[:, t, :].rearrange("p (a h e two) -> p a h e two", a=2, h=H, two=2)
                dst = partner[:, t, :].rearrange("p (a h e two) -> p a h e two", a=2, h=H, two=2)
                st = sin_t[:, t].rearrange("p a (e two) -> p a e two", two=2)
                for a in range(2):
                    for odd in range(2):
                        last = v.tensor_tensor(dst[:, a, :, :, odd], sw[:, a, :, :, 1 - odd],
                                               st[:, a:a + 1, :, odd].to_broadcast([P, H, DH // 2]), ALU.mult)
                last.then_inc(swap_done, 1)
            for t in range(NT):
                src = qk_next[:, t, :].rearrange("p (a h d) -> p a h d", a=2, h=H)
                dve.wait_ge(swap_done, t + 1)
                for a in range(2):
                    last = v.tensor_tensor(src[:, a], src[:, a], cos_t[:, t, a:a + 1, :].to_broadcast([P, H, DH]),
                                           ALU.mult)
                last.then_inc(partner_done, 1)

        def add_partners(pool):
            for t in range(NT):
                pool.wait_ge(partner_done, t + 1)
                nc.gpsimd.tensor_tensor(qk_next[:, t, :], qk_next[:, t, :], partner[:, t, :],
                                        ALU.add).then_inc(rope_done, 1)

        def project_v(pe, which, i):
            o = t_slot(slots[which, "v"][i])
            for j in range(2):
                t = 2 * i + j
                last = product(o[:, j * D:(j + 1) * D], [(xnT[:, c, t * P:(t + 1) * P], wva[:, c, :]) for c in range(NC)])
            last.then_inc(t_full, 1)

        def move_v(act, which, i):
            n = slots[which, "v"][i]
            act.wait_ge(t_full, n + 1)
            for j in range(2):
                last = nc.scalar.activation(v_places(Vpad, 2 * i + j), v_heads(t_bank(n)[:, j * D:(j + 1) * D]), ACT.Copy)
            last.then_inc(t_used, 1)

        def turn_qk(pe, which, c):
            o = t_slot(slots[which, "qkT", c])
            pe.wait_ge(rope_done, NT)
            for t in range(NT):
                last = nc.tensor.transpose(o[:, t * P:(t + 1) * P], qk_next[:, t, c * P:(c + 1) * P], ident[:])
            last.then_inc(t_full, 1)

        def move_turned(act, which, c):
            n = slots[which, "qkT", c]
            act.wait_ge(t_full, n + 1)
            nc.scalar.activation(QTa[:, c, :] if c < 2 else KTa[:, c - 2, :], t_bank(n), ACT.Copy).then_inc(t_used, 1)

        with nc.Block() as first:
            @first.sync
            def _(sp):
                sp.dma_start(xin[:], xv[0]).then_inc(x_loaded, 16)
                for dst, src in ((wqk, wqk_a), (cos_t, cos_in), (sin_t, sin_in), (wva, wv_a), (head_mask, head_mask_in),
                                 (woa, wo_a), (wg, wg_f), (wqf, wq_f), (wkf, wk_f), (wvf, wv_f), (wof, wo_f)):
                    sp.dma_start(dst[:], src).then_inc(w_early, 16)
                sp.dma_start(wb[:], w_b).then_inc(w_late, 16)
                sp.dma_start(wob[:], wo_b).then_inc(w_late, 16)
                sp.sem_inc(x_stored, 16)
                sp.wait_ge(w_early, W_EARLY)

            @first.gpsimd
            def _(pool):
                g = nc.gpsimd
                steps = [0]

                def then(ins):
                    steps[0] += 1
                    ins.then_inc(const_step, 1)
                    pool.wait_ge(const_step, steps[0])

                then(g.memset(ident[:], 0.0))
                g.affine_select(out=ident[:], in_=ident[:], compare_op=ALU.not_equal, fill=1.0, base=0,
                                pattern=[[-1, P]], channel_multiplier=1).then_inc(consts, 1)
                then(g.memset(hide[:], 0.0))
                g.affine_select(out=hide[:, T - P:T], in_=hide[:, T - P:T], compare_op=ALU.is_ge, fill=FAR, base=0,
                                pattern=[[-1, P]], channel_multiplier=1).then_inc(consts, 1)
                then(g.memset(before[:], 1.0))
                g.affine_select(out=before[:], in_=before[:], compare_op=ALU.is_gt, fill=0.0, base=0,
                                pattern=[[1, P]], channel_multiplier=-1).then_inc(consts, 1)
                g.memset(ones[:], 1.0).then_inc(consts, 1)
                g.memset(pow_half[:], -0.5).then_inc(consts, 1)
                g.memset(Vpad[:], 0.0).then_inc(consts, 1)
                g.memset(Vf[:], 0.0).then_inc(consts, 1)
                g.iota(slot_row[:], pattern=[[1, CAP]], base=0, channel_multiplier=0,
                       allow_small_or_imprecise_dtypes=True).then_inc(consts, 1)
                for s in range(NS):
                    g.iota(slot_col[:, s:s + 1], pattern=[[1, 1]], base=P * s, channel_multiplier=1,
                           allow_small_or_imprecise_dtypes=True).then_inc(consts, 1)
                pool.wait_ge(consts, CONSTS)

        with nc.Block() as start:
            @start.vector
            def _(dve):
                dve.wait_ge(x_loaded, 16)
                for i in range(2):
                    moments(dve, "first", xin, i)
                for i in range(2):
                    normalise(dve, "first", xin, xn_next, i)
                rotate(dve, "first")

            @start.gpsimd
            def _(pool):
                inverse_deviations(pool, "first")
                add_partners(pool)

            @start.tensor
            def _(pe):
                transpose_input(pe, "first", "first", xn_next)
                project_qk(pe, "first", range(NT))
                for i in range(2):
                    project_v(pe, "first", i)
                for c in range(4):
                    turn_qk(pe, "first", c)

            @start.scalar
            def _(act):
                move_input(act, "first")
                move_qk(act, "first", range(NT))
                for i in range(2):
                    move_v(act, "first", i)
                for c in range(4):
                    move_turned(act, "first", c)

        nc.all_engine_barrier(sems_to_clear=batch_sems)
        with nc.Fori(0, B) as it:
            with nc.Block(no_gpsimd_drain=True) as block:
                @block.sync
                def _(sp):
                    def load_band(n):
                        sp.dma_start(band[:, n % BANDS, :], band_in[n]).then_inc(band_loaded[n % BANDS], 16)

                    for n in range(BANDS):
                        load_band(n)
                    sp.wait_ge(s_used, slots[0, "y"][-1] + 1)
                    sp.dma_start(xin[:], xv[(it + 1) % B]).then_inc(x_loaded, 16)
                    for n in range(BANDS, H):
                        sp.wait_ge(s_used, slots[LAYERS.index(BIASED), "scores", n - BANDS][-1] + 1)
                        load_band(n)
                    sp.wait_ge(x_done, 1)
                    sp.dma_start(ov[it], x[:]).then_inc(x_stored, 16)

                @block.gpsimd
                def _(pool):
                    g = nc.gpsimd

                    for l, layer in enumerate(LAYERS):
                        if l == NL - 1:
                            inverse_deviations(pool, "next")
                        if l > 0:
                            inverse_deviations(pool, l)
                        if l == NL - 1:
                            add_partners(pool)
                        for what, n in layer_steps(l):
                            if what == "mask":
                                if n == 0 and layer is FFN:
                                    pool.wait_ge(t_used, slots[l, "q"][1] + 1)
                                if n >= Q_HELD[layer]:
                                    pool.wait_ge(s_full, slots[l, "scores", n - Q_HELD[layer]][-1] + 1)
                                src = QTa[:, n // 8, :] if layer is CAUSAL else QTf[:, n // 8, :]
                                dst = Qm[:, n % 4, :] if layer is CAUSAL else Qmf[:, n % 8, :]
                                g.tensor_scalar(dst, src, head_mask[:, n % 8:n % 8 + 1], 1.0, ALU.mult,
                                                ALU.mult).then_inc(mask_done, 1)
                            if what == "pair":
                                pool.wait_ge(t_used, slots[l, "pair", n][1] + 1)
                                for e in range(2):
                                    g.tensor_scalar(Kparts[:, n % 2, e, 0, :], KT[:, e, :], 1.0, 1.0, ALU.mult,
                                                    ALU.mult).then_inc(k_high_done, 1)
                                for e in range(2):
                                    pool.wait_ge(k_high_done, 2 * n + e + 1)
                                    g.tensor_tensor(Kparts[:, n % 2, e, 1, :], KT[:, e, :],
                                                    Kparts[:, n % 2, e, 0, :].bitcast(F32),
                                                    ALU.subtract).then_inc(k_parts_done, 1)
                            if what == "norm" and not norms[l, n][0]:
                                h = n
                                pool.wait_ge(rtotal_done, heads_before[l] + h + 1)
                                for q in range(len(widths(layer))):
                                    last = g.tensor_scalar(unit(l, h, q), unit(l, h, q), rtotal[:, h % 8, q:q + 1], 1.0,
                                                           ALU.mult, ALU.mult)
                                last.then_inc(norm_done, 1)

                @block.scalar
                def _(act):
                    a = nc.scalar

                    def full(n):
                        act.wait_ge(t_full, n + 1)

                    def exps(l, h):
                        layer = LAYERS[l]
                        for q in range(len(widths(layer))):
                            slot = slots[l, "scores", h][0 if layer is FFN else q]
                            if layer is BIASED:
                                if q == 0:
                                    act.wait_ge(peak_done, h + 1)
                            elif layer is CAUSAL or q == 0:
                                act.wait_ge(s_used, slot + 1)
                            a.activation(unit(l, h, q), unit(l, h, q), ACT.Exp, bias=peak[:, h % 8, q:q + 1],
                                         scale=1.0 if layer is BIASED else -1.0,
                                         accum_out=total[:, h % 8, q:q + 1]).then_inc(exp_done, 1)

                    for l, layer in enumerate(LAYERS):
                        if layer is BIASED:
                            move_input(act, l)
                        if l == NL - 1:
                            move_input(act, "next")
                        if layer is FFN:
                            act.wait_ge(logit_done, ffn_no[l] + 1)
                            a.activation(gate[:], z[:], ACT.Exp, scale=-1.0).then_inc(sig_exp_done, 1)
                            if l == NL - 1:
                                move_qk(act, "next", range(NT))
                                move_v(act, "next", 0)
                            n = slots[l, "gather"]
                            full(n)
                            a.activation(xgT, t_bank(n).rearrange("p (c n) -> p c n", c=NC), ACT.Copy).then_inc(t_used, 1)
                            if l == NL - 1:
                                move_v(act, "next", 1)
                            for m in range(2):
                                n = slots[l, "q"][m]
                                full(n)
                                a.activation(QTf[:, m, :], t_bank(n)[:, 0:CAP], ACT.Copy,
                                             scale=-float(DH) ** -0.5).then_inc(t_used, 1)
                            n = slots[l, "k"]
                            full(n)
                            a.activation(KTf, t_bank(n).rearrange("p (c n) -> p c n", c=2), ACT.Copy).then_inc(t_used, 1)
                        for what, n in layer_steps(l):
                            if what == "pair":
                                _, ks, vs = slots[l, "pair", n]
                                full(ks)
                                if n > 0:
                                    act.wait_ge(k_parts_done, 2 * n)
                                for e in range(2):
                                    for half in range(2):
                                        last = a.activation(KT[half * DB:(half + 1) * DB, e, :],
                                                            t_bank(ks)[e * DB:(e + 1) * DB, :], ACT.Copy)
                                last.then_inc(t_used, 1)
                                full(vs)
                                if n >= 4:
                                    act.wait_ge(s_full, slots[l, "values", n - 4] + 1)
                                a.activation(Vb[:, n % 4], t_bank(vs).rearrange("p (t n) -> p t n", t=NT),
                                             ACT.Copy).then_inc(t_used, 1)
                            if what == "norm" and norms[l, n][0]:
                                act.wait_ge(rtotal_done, heads_before[l] + n + 1)
                                for q in range(len(widths(layer))):
                                    last = a.activation(unit(l, n, q), unit(l, n, q), ACT.Copy,
                                                        scale=rtotal[:, n % 8, q:q + 1])
                                last.then_inc(scalar_norm_done, 1)
                            if what == "next_turn":
                                move_turned(act, "next", n)
                            if what == "scores":
                                exps(l, n)
                            if what == "turn" and any(ring == "t" for ring, _ in slots[l, "turn", n]):
                                old = n - PT_HELD[layer]
                                if old >= 0:
                                    act.wait_ge(s_full, slots[l, "values", old // GROUP[layer]] + 1)
                                for k, (ring, m) in enumerate(slots[l, "turn", n]):
                                    if ring == "t":
                                        full(m)
                                        lo = k * P if layer is CAUSAL else 0
                                        a.activation(turned(l, n, k), t_bank(m)[:, lo:T], ACT.Copy).then_inc(t_used, 1)
                        if layer is FFN:
                            n = slots[l, "o"]
                            full(n)
                            a.activation(of, t_bank(n).rearrange("p (s n) -> p s n", s=NS), ACT.Copy).then_inc(t_used, 1)

                @block.vector
                def _(dve):
                    v = nc.vector

                    def full(n):
                        dve.wait_ge(s_full, n + 1)

                    def layer_norm(l, i):
                        normalise(dve, l, x, xn, i)
                        if LAYERS[l] is FFN:
                            dve.wait_ge(xn_done, 2 * norm_no[l] + i + 1)
                            for t in range(2 * i, 2 * i + 2):
                                last = v.tensor_tensor_reduce(out=logit_products[:, t, :], in0=xn[:, t, :], in1=wg[:],
                                                              scale=1.0, scalar=0.0, op0=ALU.mult, op1=ALU.add,
                                                              accum_out=z[:, t:t + 1])
                            if i == 1:
                                last.then_inc(logit_done, 1)

                    for l, layer in enumerate(LAYERS):
                        if layer is FFN:
                            f = ffn_no[l]
                            dve.wait_ge(sig_exp_done, f + 1)
                            v.tensor_scalar_add(z[:], gate[:], 1.0).then_inc(sig_sum_done, 1)
                            dve.wait_ge(sig_sum_done, f + 1)
                            v.reciprocal(gate[:], z[:]).then_inc(gate_done, 1)
                            n = slots[l, "row"]
                            full(n)
                            v.tensor_copy(gate_row[:], s_bank(n)).then_inc(s_used, 1)
                            dve.wait_ge(s_used, n + 1)
                            for t in range(NT):
                                own = slice(t * P, (t + 1) * P)
                                v.scalar_tensor_tensor(out=tie[:, t, :], in0=gate_row[:, own], scalar=gate[:, t:t + 1],
                                                       in1=before[:], op0=ALU.is_equal, op1=ALU.mult)
                            for t in range(NT):
                                last = v.tensor_scalar(above[:, t, 0:(t + 1) * P], gate_row[:, 0:(t + 1) * P],
                                                       gate[:, t:t + 1], None, ALU.is_lt)
                                if t < NT - 1:
                                    v.tensor_scalar(above[:, t, (t + 1) * P:T], gate_row[:, (t + 1) * P:T],
                                                    gate[:, t:t + 1], None, ALU.is_le)
                            last.then_inc(above_done, 1)
                            cn, rn = slots[l, "rank"]
                            full(cn)
                            v.tensor_copy(rank[:], s_bank(cn)[:, 0:NT]).then_inc(s_used, 1)
                            dve.wait_ge(s_used, cn + 1)
                            for t in range(NT):
                                last = v.tensor_scalar(pick[:, t, :], slot_row[:], rank[:, t:t + 1], None, ALU.is_equal)
                            last.then_inc(pick_done, 1)
                            full(rn)
                            for s in range(NS):
                                last = v.scalar_tensor_tensor(out=spread[:, s, :], in0=s_bank(rn),
                                                              scalar=slot_col[:, s:s + 1], in1=gate_row[:],
                                                              op0=ALU.is_equal, op1=ALU.mult)
                            last.then_inc(s_used, 1)
                            if l == NL - 1:
                                rotate(dve, "next")
                            n = slots[l, "v"]
                            full(n)
                            for s in range(NS):
                                last = v.tensor_copy(v_places(Vf, s), v_heads(s_bank(n)[:, s * D:(s + 1) * D]))
                            last.then_inc(s_used, 1)

                        def inverse(h):
                            dve.wait_ge(exp_done, units_before[l] + (h + 1) * len(widths(layer)))
                            w = len(widths(layer))
                            v.reciprocal(rtotal[:, h % 8, 0:w], total[:, h % 8, 0:w]).then_inc(rtotal_done, 1)

                        for what, n in layer_steps(l):
                            if what == "pair":
                                m = slots[l, "pair", n][0]
                                full(m)
                                for e in range(2):
                                    rows = slice(e * DB, (e + 1) * DB)
                                    v.tensor_scalar(Qparts[rows, (2 * n + e) % 4, :], s_bank(m)[rows, :], float(DB) ** -0.5,
                                                    None, ALU.mult).then_inc(q_high_done, 1)
                                for e in range(2):
                                    rows, others = slice(e * DB, (e + 1) * DB), slice((1 - e) * DB, (2 - e) * DB)
                                    dve.wait_ge(q_high_done, 2 * n + e + 1)
                                    last = v.scalar_tensor_tensor(out=Qparts[others, (2 * n + e) % 4, :],
                                                                  in0=s_bank(m)[rows, :], scalar=float(DB) ** -0.5,
                                                                  in1=Qparts[rows, (2 * n + e) % 4, :].bitcast(F32),
                                                                  op0=ALU.mult, op1=ALU.subtract)
                                last.then_inc(s_used, 1)
                            if what == "scores":
                                if n >= HELD[layer]:
                                    ring, m = slots[l, "turn", n - HELD[layer]][-1]
                                    dve.wait_ge(s_full if ring == "s" else t_full, m + 1)
                                if layer is BIASED:
                                    dve.wait_ge(band_loaded[n % BANDS], 16 * (n // BANDS + 1))
                                for q, w in enumerate(widths(layer)):
                                    m = slots[l, "scores", n][0 if layer is FFN else q]
                                    if layer is not FFN or q == 0:
                                        dve.wait_ge(s_full, m + 1)
                                    if layer is FFN:
                                        src, add = s_bank(m)[:, q * CAP:(q + 1) * CAP], hide[:, 0:CAP]
                                    elif layer is CAUSAL:
                                        src, add = s_bank(m)[:, 0:w], hide[:, T - w:T]
                                    else:
                                        lo = (NT - 1 - q) * P
                                        src, add = s_bank(m), band[:, n % BANDS, lo:lo + T]
                                    sign = 1 if layer is BIASED else -1
                                    last = v.tensor_tensor_reduce(out=unit(l, n, q), in0=src, in1=add, scale=1.0,
                                                                  scalar=-sign * 3e38, op0=ALU.add,
                                                                  op1=ALU.max if layer is BIASED else ALU.min,
                                                                  accum_out=peak[:, n % 8, q:q + 1])
                                    if layer is not FFN or q == NS - 1:
                                        last.then_inc(s_used, 1)
                                if layer is BIASED:
                                    dve.wait_ge(s_used, slots[l, "scores", n][-1] + 1)
                                    v.tensor_scalar(peak[:, n % 8, :], peak[:, n % 8, :], -1.0, None,
                                                    ALU.mult).then_inc(peak_done, 1)
                            if what == "norm":
                                inverse(n)
                            if what == "turn" and any(ring == "s" for ring, _ in slots[l, "turn", n]):
                                old = n - PT_HELD[layer]
                                if old >= 0:
                                    dve.wait_ge(s_full, slots[l, "values", old // GROUP[layer]] + 1)
                                for k, (ring, m) in enumerate(slots[l, "turn", n]):
                                    if ring == "s":
                                        full(m)
                                        lo = k * P if layer is CAUSAL else 0
                                        v.tensor_copy(turned(l, n, k), s_bank(m)[:, lo:T]).then_inc(s_used, 1)
                            if what == "values":
                                m = slots[l, "values", n]
                                full(m)
                                src = s_bank(m)[:, 0:CAP if layer is FFN else T]
                                if layer is BIASED:
                                    v.tensor_copy(OTb[:, n, :], src).then_inc(s_used, 1)
                                else:
                                    dst = (OTa if layer is CAUSAL else OTf)[:, n // 2, :]
                                    if n % 2 == 0:
                                        v.tensor_copy(dst, src).then_inc(s_used, 1)
                                    else:
                                        dve.wait_ge(s_used, slots[l, "values", n - 1] + 1)
                                        v.tensor_tensor(dst, dst, src, ALU.add).then_inc(s_used, 1)

                        if l == NL - 2:
                            dve.wait_ge(x_loaded, it * 16 + 32)
                            for i in range(2):
                                moments(dve, "next", xin, i)
                            for i in range(2):
                                normalise(dve, "next", xin, xn_next, i)
                        for i in range(NT // 2):
                            n = slots[l, "y"][i]
                            full(n)
                            if l == 0:
                                dve.wait_ge(x_stored, it * 16 + 16)
                            last = v.tensor_tensor(x[:, 2 * i:2 * i + 2, :], (xin if l == 0 else x)[:, 2 * i:2 * i + 2, :],
                                                   s_bank(n).rearrange("p (t d) -> p t d", t=2), ALU.add)
                            last.then_inc(s_used, 1)
                            if l < NL - 1:
                                dve.wait_ge(s_used, n + 1)
                                moments(dve, l + 1, x, i)
                        if l < NL - 1:
                            for i in range(2):
                                layer_norm(l + 1, i)
                    dve.wait_ge(s_used, slots[NL - 1, "y"][-1] + 1)
                    dve.sem_inc(x_done, 1)

                @block.tensor
                def _(pe):
                    te = nc.tensor

                    def keep_warm(o, why):
                        for _ in range(WARM[why]):
                            te.matmul(o, ident[:], hide[:], start=True, stop=True)

                    def s_ready(n):
                        pe.wait_ge(s_used, n + 1)

                    def t_ready(n):
                        pe.wait_ge(t_used, n + 1)

                    for l, layer in enumerate(LAYERS):
                        if layer is BIASED:
                            keep_warm(t_slot(slots[l, "xT"][0]), "input")
                            transpose_input(pe, l, l, xn)
                            t_ready(slots[l, "xT"][-1])
                        if l == NL - 1:
                            transpose_input(pe, "next", "next", xn_next)
                            project_qk(pe, "next", range(2))
                        if layer is FFN:
                            f = ffn_no[l]
                            o = s_slot(slots[l, "row"])
                            if l < NL - 1:
                                keep_warm(o, "gates")
                            pe.wait_ge(gate_done, f + 1)
                            for t in range(NT):
                                last = te.transpose(o[:, t * P:(t + 1) * P], gate[:, t:t + 1].to_broadcast([P, P]), ident[:])
                            last.then_inc(s_full, 1)
                            if l == NL - 1:
                                project_qk(pe, "next", range(2, NT))
                            if l < NL - 1:
                                keep_warm(s_slot(slots[l, "rank"][0]), "ranks")
                            pe.wait_ge(above_done, f + 1)
                            cn, rn = slots[l, "rank"]
                            o = s_slot(cn)
                            for i in range(NT):
                                own = slice(i * P, (i + 1) * P)
                                last = product(o[:, i:i + 1], [(tie[:, i, :], ones[:, 0:1])] +
                                               [(above[:, t, own], ones[:, 0:1]) for t in range(NT)])
                            last.then_inc(s_full, 1)
                            o = s_slot(rn)
                            for t in range(NT):
                                last = te.matmul(o, ones[:], above[:, t, :], start=(t == 0), stop=(t == NT - 1))
                                if t == 0:
                                    for i in range(NT):
                                        te.matmul(o[:, i * P:(i + 1) * P], ones[:], tie[:, i, :], start=False, stop=False)
                            last.then_inc(s_full, 1)
                            if l == NL - 1:
                                project_v(pe, "next", 0)
                            pe.wait_ge(pick_done, f + 1)
                            o = t_slot(slots[l, "gather"])
                            for c in range(NC):
                                last = product(o[:, c * CAP:(c + 1) * CAP], [(xn[:, t, c * P:(c + 1) * P], pick[:, t, :])
                                                                             for t in range(NT)])
                            last.then_inc(t_full, 1)
                            if l == NL - 1:
                                project_v(pe, "next", 1)
                            t_ready(slots[l, "gather"])
                            for m in range(2):
                                product(t_slot(slots[l, "q"][m])[:, 0:CAP],
                                        [(wqf[:, c, m * P:(m + 1) * P], xgT[:, c, :]) for c in range(NC)]).then_inc(t_full, 1)
                            o = t_slot(slots[l, "k"])
                            for m in range(2):
                                last = product(o[:, m * CAP:(m + 1) * CAP],
                                               [(wkf[:, c, m * P:(m + 1) * P], xgT[:, c, :]) for c in range(NC)])
                            last.then_inc(t_full, 1)
                            o = s_slot(slots[l, "v"])
                            for s in range(NS):
                                last = product(o[:, s * D:(s + 1) * D],
                                               [(xgT[:, c, s * P:(s + 1) * P], wvf[:, c, :]) for c in range(NC)])
                            last.then_inc(s_full, 1)
                            t_ready(slots[l, "k"])

                        for what, n in layer_steps(l):
                            if what == "pair":
                                if n == 0:
                                    pe.wait_ge(w_late, W_LATE)
                                qs, ks, vs = slots[l, "pair", n]
                                product(t_slot(ks), [(wb[:, c, 1, n * P:(n + 1) * P], xnT[:, c, :])
                                                     for c in range(NC)]).then_inc(t_full, 1)
                                product(s_slot(qs), [(wb[:, c, 0, n * P:(n + 1) * P], xnT[:, c, :])
                                                     for c in range(NC)]).then_inc(s_full, 1)
                                o = t_slot(vs)
                                for t in range(NT):
                                    last = product(o[:, t * P:(t + 1) * P],
                                                   [(xnT[:, c, t * P:(t + 1) * P], wb[:, c, 2, n * P:(n + 1) * P])
                                                    for c in range(NC)])
                                last.then_inc(t_full, 1)
                            if what == "next_turn":
                                turn_qk(pe, "next", n)
                            if what == "scores":
                                if layer is BIASED:
                                    s_ready(slots[l, "pair", n // 2][0])
                                    pe.wait_ge(k_parts_done, n + 1)
                                else:
                                    pe.wait_ge(mask_done, mask_before[l] + n + 1)
                                    keys = KTa[:, n // 8, :] if layer is CAUSAL else KTf[:, n // 8, :]
                                for q, w in enumerate(widths(layer)):
                                    m = slots[l, "scores", n][0 if layer is FFN else q]
                                    if layer is FFN:
                                        o = (s_slot(m) if q == 0 else s_bank(m))[:, q * CAP:(q + 1) * CAP]
                                    else:
                                        o = s_slot(m)[:, 0:w]
                                    rows = slice(q * P, (q + 1) * P)
                                    if layer is BIASED:
                                        last = product(o, [(Qparts[:, n % 4, rows], Kparts[:, (n // 2) % 2, n % 2, part, :])
                                                           for part in range(2)])
                                    else:
                                        qs = Qmf[:, n % 8, :] if layer is FFN else Qm[:, n % 4, :]
                                        last = te.matmul(o, qs[:, rows], keys[:, 0:w], start=True, stop=True)
                                    if layer is not FFN or q == NS - 1:
                                        last.then_inc(s_full, 1)
                            if what == "turn":
                                by_scalar, count = norms[l, n]
                                pe.wait_ge(scalar_norm_done if by_scalar else norm_done, count)
                                for k, (ring, m) in enumerate(slots[l, "turn", n]):
                                    o = s_slot(m) if ring == "s" else t_slot(m)
                                    if layer is FFN:
                                        blocks = [(q, i) for i in range(NS) for q in range(NS)]
                                    else:
                                        blocks = [(q, k) for q in range(k if layer is CAUSAL else 0, NT)]
                                    for q, i in blocks:
                                        at = (i * CAP if layer is FFN else 0) + q * P
                                        last = te.transpose(o[:, at:at + P], unit(l, n, q)[:, i * P:(i + 1) * P],
                                                            ident[:])
                                    last.then_inc(s_full if ring == "s" else t_full, 1)
                            if what == "values":
                                size = GROUP[layer]
                                heads = range(size * n, size * n + size)
                                for ring in "st":
                                    m = [m for h in heads for r, m in slots[l, "turn", h] if r == ring]
                                    if m:
                                        (s_ready if ring == "s" else t_ready)(m[-1])
                                m = slots[l, "values", n]
                                o = s_slot(m)
                                if layer is BIASED:
                                    t_ready(slots[l, "pair", n][2])
                                if layer is FFN and n == 0:
                                    s_ready(slots[l, "v"])
                                rows = P // size
                                for k in range(NS if layer is FFN else NT):
                                    for e, h in enumerate(heads):
                                        lo = k * P if layer is CAUSAL else 0
                                        hi = CAP if layer is FFN else T
                                        if layer is BIASED:
                                            w = Vb[:, n % 4, k, e * DB:(e + 1) * DB]
                                        else:
                                            w = v_head(Vf if layer is FFN else Vpad, k, h)
                                        last = te.matmul(o[e * rows:(e + 1) * rows, lo:hi], w, pt(l, h, k), start=(k == 0),
                                                         stop=(k == (NS if layer is FFN else NT) - 1))
                                last.then_inc(s_full, 1)

                        def sums(o, parts, count, before_last=None):
                            for k in range(count):
                                if k == count - 1 and before_last is not None:
                                    s_ready(before_last)
                                for j in range(2):
                                    w, r = parts(j, k)
                                    last = te.matmul(o[:, j * D:(j + 1) * D], w, r, start=(k == 0 and j == 0),
                                                     stop=(k == count - 1 and j == 1))
                            return last

                        last_group = slots[l, "values", H // GROUP[layer] - 1]
                        s_ready(slots[l, "values", H // GROUP[layer] - (2 if layer is BIASED else 3)])
                        if layer is FFN:
                            sums(t_slot(slots[l, "o"]), lambda s, g: (OTf[:, g, s * P:(s + 1) * P], wof[:, g, :]), NC,
                                 last_group).then_inc(t_full, 1)
                            t_ready(slots[l, "o"])
                        for i in range(NT // 2):
                            o = s_slot(slots[l, "y"][i])

                            def tokens(j):
                                return slice((2 * i + j) * P, (2 * i + j + 1) * P)

                            if layer is FFN:
                                last = sums(o, lambda j, s: (spread[:, s, tokens(j)], of[:, s, :]), NS)
                            else:
                                heads, w = (OTa, woa) if layer is CAUSAL else (OTb, wob)
                                last = sums(o, lambda j, g: (heads[:, g, tokens(j)], w[:, g, :]),
                                            H * DB // P if layer is BIASED else NC,
                                            last_group if i == 0 else None)
                            last.then_inc(s_full, 1)


            nc.all_engine_barrier(sems_to_clear=batch_sems)
        with nc.Block() as end:

            @end.sync
            def _(sp):
                sp.wait_ge(x_stored, 16 * (B + 1))
                sp.wait_ge(x_loaded, 16 * (B + 1))


def kernel(L0_attn_a_x, L0_attn_a_Wq, L0_attn_a_Wk, L0_attn_a_Wv, L0_attn_a_Wo, L0_attn_b_w_qkv, L0_attn_b_w_out,
           L0_attn_b_rel_bias, L0_ffn_Wg, L0_ffn_Wq, L0_ffn_Wk, L0_ffn_Wv, L0_ffn_Wo):
    import numpy as np
    import concourse.bacc as bacc
    from concourse.bass_utils import run_bass_kernel_spmd

    def chunks(w):
        w = np.asarray(w)
        return np.ascontiguousarray(w.reshape(-1, P, w.shape[-1]).transpose(1, 0, 2))

    def by_groups(w):
        w = np.asarray(w)
        return w.reshape(D, 2, 2, 4, DH).transpose(0, 2, 1, 3, 4).reshape(D, D)

    def by_pairs(w):
        w = np.asarray(w)
        return w.reshape(2, 2, 4, DH, D).transpose(0, 2, 1, 3, 4).reshape(D, D)

    inv = np.float32(10000.0) ** (-(np.arange(DH // 2, dtype=np.float32) * np.float32(2.0 / DH)))
    angle = np.arange(T, dtype=np.float32)[:, None] * inv[None, :].astype(np.float32)
    cos = np.repeat(np.cos(angle), 2, axis=1).astype(np.float32)
    sin = np.stack([-np.sin(angle), np.sin(angle)], axis=-1).reshape(T, DH).astype(np.float32)
    scale = np.array([-float(DH) ** -0.5, 1.0], np.float32)[None, :, None]
    cos2 = np.ascontiguousarray((cos[:, None, :] * scale).reshape(NT, P, 2, DH).transpose(1, 0, 2, 3))
    sin2 = np.ascontiguousarray((sin[:, None, :] * scale).reshape(NT, P, 2, DH).transpose(1, 0, 2, 3))
    head_mask = (np.arange(P)[:, None] // DH == np.arange(8)[None, :]).astype(np.float32)
    at = np.minimum(np.arange(BAND)[None, :] - np.arange(P)[:, None] + P - 1, REL - 1)
    band = np.ascontiguousarray(np.asarray(L0_attn_b_rel_bias).T[:, at])

    w_b = np.asarray(L0_attn_b_w_qkv).reshape(DB, 3, H, D).transpose(3, 1, 2, 0).reshape(D, 3 * H * DB)
    w_b = chunks(w_b).reshape(P, NC, 3, H * DB)
    wqk_a = chunks(np.concatenate([np.asarray(L0_attn_a_Wq).T, np.asarray(L0_attn_a_Wk).T], axis=1))
    arrays = {
        "x": np.asarray(L0_attn_a_x),
        "wqk_a": wqk_a,
        "wv_a": chunks(by_groups(np.asarray(L0_attn_a_Wv).T)),
        "wo_a": chunks(by_pairs(np.asarray(L0_attn_a_Wo).T)),
        "w_b": w_b,
        "wo_b": chunks(np.asarray(L0_attn_b_w_out).T),
        "band": band,
        "wg_f": np.ascontiguousarray(np.broadcast_to(np.asarray(L0_ffn_Wg).reshape(1, D), (P, D))),
        "wq_f": chunks(L0_ffn_Wq),
        "wk_f": chunks(L0_ffn_Wk),
        "wv_f": chunks(by_groups(L0_ffn_Wv)),
        "wo_f": chunks(by_pairs(L0_ffn_Wo)),
        "cos": cos2,
        "sin": sin2,
        "head_mask": head_mask,
    }
    nc = bacc.Bacc("TRN2", target_bir_lowering=False, num_devices=1)
    ins = {f"in_{k}": np.ascontiguousarray(a) for k, a in arrays.items()}
    aps = [nc.dram_tensor(k, a.shape, mybir.dt.from_np(a.dtype), kind="ExternalInput").ap() for k, a in ins.items()]
    out = nc.dram_tensor("out", (B, T, D), F32, kind="ExternalOutput").ap()
    hybrid_kernel(nc, *aps, out)
    r = run_bass_kernel_spmd(nc, [ins], core_ids=[0])
    return r.results[0]["out"]
```
